# Optimizing a Trainium2 kernel written in Bass

```python
import numpy as np
import jax
import jax.numpy as jnp

def _softmax(x, axis=-1):
    return jax.nn.softmax(x, axis=axis)

def _gelu(x):
    return jax.nn.gelu(x, approximate=True)

def _silu(x):
    return jax.nn.silu(x)

def _sigmoid(x):
    return jax.nn.sigmoid(x)

def _layernorm(x, axis=-1, eps=1e-05):
    m = jnp.mean(x, axis=axis, keepdims=True)
    v = jnp.var(x, axis=axis, keepdims=True)
    return (x - m) / jnp.sqrt(v + eps)

def _scatter_add(tgt, idx, src, axis=0):
    return tgt.at[idx].add(src)

def _segment_sum(src, seg, n):
    return jax.ops.segment_sum(src, seg, n)
kernel_name = 'mk_macaron_d2_jaxref_r8_340bd6'

def setup_inputs(seed: int=0):
    np.random.seed(seed)
    _w = jnp.asarray

    def _L0_attn_setup():
        import jax, jax.numpy as jnp
        from jax import lax
        import numpy as np
        D_MODEL, D_INNER, D_STATE, D_CONV, DT_RANK = (256, 512, 16, 4, 128)
        B, L = (2, 128)
        key = jax.random.key(seed)
        ks = jax.random.split(key, 10)
        s = 0.02
        x = jax.random.normal(ks[0], (B, L, D_MODEL), jnp.float32)
        W_in = jax.random.normal(ks[1], (2 * D_INNER, D_MODEL), jnp.float32) * s
        conv_w = jax.random.normal(ks[2], (D_INNER, D_CONV), jnp.float32) * s
        conv_b = jax.random.normal(ks[3], (D_INNER,), jnp.float32) * s
        W_x = jax.random.normal(ks[4], (DT_RANK + 2 * D_STATE, D_INNER), jnp.float32) * s
        W_dt = jax.random.normal(ks[5], (D_INNER, DT_RANK), jnp.float32) * s
        b_dt = jax.random.normal(ks[6], (D_INNER,), jnp.float32) * s
        A_log = jnp.log(jnp.broadcast_to(jnp.arange(1, D_STATE + 1, dtype=jnp.float32), (D_INNER, D_STATE)))
        Dp = jnp.ones((D_INNER,), jnp.float32)
        W_out = jax.random.normal(ks[7], (D_MODEL, D_INNER), jnp.float32) * s
        return {'x': x, 'W_in': W_in, 'conv_w': conv_w, 'conv_b': conv_b, 'W_x': W_x, 'W_dt': W_dt, 'b_dt': b_dt, 'A_log': A_log, 'Dp': Dp, 'W_out': W_out}
    _L0_attn_in = _L0_attn_setup()

    def _L0_ffn_setup():
        import jax, jax.numpy as jnp
        import numpy as np
        B, S, D, H = (4, 256, 256, 1024)

        def fwht(x):
            orig_shape = x.shape
            n = orig_shape[-1]
            x = x.reshape(-1, n)
            h = 1
            while h < n:
                xb = x.reshape(-1, n // (2 * h), 2, h)
                a = xb[:, :, 0, :]
                b = xb[:, :, 1, :]
                x = jnp.stack([a + b, a - b], axis=2).reshape(-1, n)
                h *= 2
            scale = jnp.asarray(1.0 / np.sqrt(n), dtype=x.dtype)
            return (x * scale).reshape(orig_shape)
        key = jax.random.key(seed)
        kx, k1, k2, k3 = jax.random.split(key, 4)
        x = jax.random.normal(kx, (B, S, D), dtype=jnp.float32)
        W1 = jax.random.normal(k1, (H, D), dtype=jnp.float32) * (1.0 / np.sqrt(D))
        W2 = jax.random.normal(k2, (D, H), dtype=jnp.float32) * (1.0 / np.sqrt(H))
        W3 = jax.random.normal(k3, (H, D), dtype=jnp.float32) * (1.0 / np.sqrt(D))
        return {'x': x, 'W1': W1, 'W2': W2, 'W3': W3}
    _L0_ffn_in = _L0_ffn_setup()

    def _L1_attn_setup():
        import jax, jax.numpy as jnp
        import numpy as np
        import math
        E = 256
        H = 16
        D = E // H

        def _alibi_slopes(n):

            def pow2_slopes(n):
                start = 2 ** (-2 ** (-(math.log2(n) - 3)))
                return [start * start ** i for i in range(n)]
            if math.log2(n).is_integer():
                return pow2_slopes(n)
            c = 2 ** math.floor(math.log2(n))
            return pow2_slopes(c) + _alibi_slopes(2 * c)[::2][:n - c]

        def _alibi_bias(seq_len):
            slopes = jnp.asarray(_alibi_slopes(H), dtype=jnp.float32)
            pos = jnp.arange(seq_len)
            rel = jnp.abs(pos[None, :] - pos[:, None]).astype(jnp.float32)
            return -slopes[:, None, None] * rel[None, :, :]
        key = jax.random.key(seed)
        ks = jax.random.split(key, 5)
        B, S = (2, 256)
        scale = 1.0 / math.sqrt(E)
        x = jax.random.normal(ks[0], (B, S, E), dtype=jnp.float32)
        Wq = jax.random.normal(ks[1], (E, E), dtype=jnp.float32) * scale
        Wk = jax.random.normal(ks[2], (E, E), dtype=jnp.float32) * scale
        Wv = jax.random.normal(ks[3], (E, E), dtype=jnp.float32) * scale
        Wo = jax.random.normal(ks[4], (E, E), dtype=jnp.float32) * scale
        z = jnp.zeros((E,), dtype=jnp.float32)
        return {'x': x, 'Wq': Wq, 'bq': z, 'Wk': Wk, 'bk': z, 'Wv': Wv, 'bv': z, 'Wo': Wo, 'bo': z}
    _L1_attn_in = _L1_attn_setup()

    def _L1_ffn_setup():
        import jax, jax.numpy as jnp
        import numpy as np
        B, S, D = (2, 256, 256)
        E, H, TOP_K = (8, 176, 2)
        SH = 176
        ROUTED_SCALE = 2.5
        key = jax.random.key(seed)
        ks = jax.random.split(key, 8)
        std = 0.02
        return {'x': jax.random.normal(ks[0], (B, S, D), jnp.float32), 'gate_w': jax.random.normal(ks[1], (E, D), jnp.float32) * std, 'w1': jax.random.normal(ks[2], (E, D, H), jnp.float32) * std, 'w3': jax.random.normal(ks[3], (E, D, H), jnp.float32) * std, 'w2': jax.random.normal(ks[4], (E, H, D), jnp.float32) * std, 'sw1': jax.random.normal(ks[5], (D, SH), jnp.float32) * std, 'sw3': jax.random.normal(ks[6], (D, SH), jnp.float32) * std, 'sw2': jax.random.normal(ks[7], (SH, D), jnp.float32) * std}
    _L1_ffn_in = _L1_ffn_setup()
    _d = {'L0_attn_x': _L0_attn_in['x'], 'L0_attn_W_in': _L0_attn_in['W_in'], 'L0_attn_conv_w': _L0_attn_in['conv_w'], 'L0_attn_conv_b': _L0_attn_in['conv_b'], 'L0_attn_W_x': _L0_attn_in['W_x'], 'L0_attn_W_dt': _L0_attn_in['W_dt'], 'L0_attn_b_dt': _L0_attn_in['b_dt'], 'L0_attn_A_log': _L0_attn_in['A_log'], 'L0_attn_Dp': _L0_attn_in['Dp'], 'L0_attn_W_out': _L0_attn_in['W_out'], 'L0_ffn_W1': _L0_ffn_in['W1'], 'L0_ffn_W2': _L0_ffn_in['W2'], 'L0_ffn_W3': _L0_ffn_in['W3'], 'L1_attn_Wq': _L1_attn_in['Wq'], 'L1_attn_bq': _L1_attn_in['bq'], 'L1_attn_Wk': _L1_attn_in['Wk'], 'L1_attn_bk': _L1_attn_in['bk'], 'L1_attn_Wv': _L1_attn_in['Wv'], 'L1_attn_bv': _L1_attn_in['bv'], 'L1_attn_Wo': _L1_attn_in['Wo'], 'L1_attn_bo': _L1_attn_in['bo'], 'L1_ffn_gate_w': _L1_ffn_in['gate_w'], 'L1_ffn_w1': _L1_ffn_in['w1'], 'L1_ffn_w2': _L1_ffn_in['w2'], 'L1_ffn_w3': _L1_ffn_in['w3'], 'L1_ffn_sw1': _L1_ffn_in['sw1'], 'L1_ffn_sw2': _L1_ffn_in['sw2'], 'L1_ffn_sw3': _L1_ffn_in['sw3']}
    _x0 = _d['L0_attn_x']
    _d['L0_attn_x'] = jax.random.normal(jax.random.fold_in(jax.random.key(seed), 1), (2, 512, 256), dtype=_x0.dtype)
    del _x0
    return _d

def reference(L0_attn_x, L0_attn_W_in, L0_attn_conv_w, L0_attn_conv_b, L0_attn_W_x, L0_attn_W_dt, L0_attn_b_dt, L0_attn_A_log, L0_attn_Dp, L0_attn_W_out, L0_ffn_W1, L0_ffn_W2, L0_ffn_W3, L1_attn_Wq, L1_attn_bq, L1_attn_Wk, L1_attn_bk, L1_attn_Wv, L1_attn_bv, L1_attn_Wo, L1_attn_bo, L1_ffn_gate_w, L1_ffn_w1, L1_ffn_w2, L1_ffn_w3, L1_ffn_sw1, L1_ffn_sw2, L1_ffn_sw3):

    def _L0_attn_ref(x, W_in, conv_w, conv_b, W_x, W_dt, b_dt, A_log, Dp, W_out):
        import jax, jax.numpy as jnp
        from jax import lax
        import numpy as np
        D_MODEL, D_INNER, D_STATE, D_CONV, DT_RANK = (256, 512, 16, 4, 128)
        B, L = (2, 128)
        b, l, _ = x.shape
        d_inner, d_state = A_log.shape
        dt_rank = W_dt.shape[1]
        d_conv = conv_w.shape[1]
        xz = jnp.einsum('bld,ed->ble', x, W_in)
        xp, z = jnp.split(xz, 2, axis=-1)
        xpad = jnp.pad(xp, ((0, 0), (d_conv - 1, 0), (0, 0)))
        xc = conv_b + sum((xpad[:, k:k + l, :] * conv_w[:, k] for k in range(d_conv)))
        xc = jax.nn.silu(xc)
        dbc = jnp.einsum('ble,fe->blf', xc, W_x)
        dt = dbc[..., :dt_rank]
        Bm = dbc[..., dt_rank:dt_rank + d_state]
        Cm = dbc[..., dt_rank + d_state:]
        delta = jax.nn.softplus(jnp.einsum('blr,er->ble', dt, W_dt) + b_dt)
        A = -jnp.exp(A_log)
        dA = jnp.exp(delta[..., None] * A)
        dBx = delta[..., None] * Bm[:, :, None, :] * xc[..., None]

        def step(h, inp):
            dA_t, dBx_t = inp
            h = dA_t * h + dBx_t
            return (h, h)
        h0 = jnp.zeros((b, d_inner, d_state), x.dtype)
        _, hs = lax.scan(step, h0, (jnp.swapaxes(dA, 0, 1), jnp.swapaxes(dBx, 0, 1)))
        hs = jnp.swapaxes(hs, 0, 1)
        y = jnp.einsum('bles,bls->ble', hs, Cm) + xc * Dp
        y = y * jax.nn.silu(z)
        return jnp.einsum('ble,de->bld', y, W_out)

    def _L0_ffn_ref(x, W1, W2, W3):
        import jax, jax.numpy as jnp
        import numpy as np
        B, S, D, H = (4, 256, 256, 1024)

        def fwht(x):
            orig_shape = x.shape
            n = orig_shape[-1]
            x = x.reshape(-1, n)
            h = 1
            while h < n:
                xb = x.reshape(-1, n // (2 * h), 2, h)
                a = xb[:, :, 0, :]
                b = xb[:, :, 1, :]
                x = jnp.stack([a + b, a - b], axis=2).reshape(-1, n)
                h *= 2
            scale = jnp.asarray(1.0 / np.sqrt(n), dtype=x.dtype)
            return (x * scale).reshape(orig_shape)
        up_gate = jnp.einsum('bsd,hd->bsh', x, W1)
        up_lin = jnp.einsum('bsd,hd->bsh', x, W3)
        hidden = jax.nn.silu(up_gate) * up_lin
        hidden = fwht(hidden)
        out = jnp.einsum('bsh,dh->bsd', hidden, W2)
        return out

    def _L1_attn_ref(x, Wq, bq, Wk, bk, Wv, bv, Wo, bo):
        import jax, jax.numpy as jnp
        import numpy as np
        import math
        E = 256
        H = 16
        D = E // H

        def _alibi_slopes(n):

            def pow2_slopes(n):
                start = 2 ** (-2 ** (-(math.log2(n) - 3)))
                return [start * start ** i for i in range(n)]
            if math.log2(n).is_integer():
                return pow2_slopes(n)
            c = 2 ** math.floor(math.log2(n))
            return pow2_slopes(c) + _alibi_slopes(2 * c)[::2][:n - c]

        def _alibi_bias(seq_len):
            slopes = jnp.asarray(_alibi_slopes(H), dtype=jnp.float32)
            pos = jnp.arange(seq_len)
            rel = jnp.abs(pos[None, :] - pos[:, None]).astype(jnp.float32)
            return -slopes[:, None, None] * rel[None, :, :]
        B, S, _ = x.shape

        def proj(W, b):
            return (x @ W.T + b).reshape(B, S, H, D).transpose(0, 2, 1, 3)
        q = proj(Wq, bq)
        k = proj(Wk, bk)
        v = proj(Wv, bv)
        scores = jnp.einsum('bhqd,bhkd->bhqk', q, k) / math.sqrt(D)
        causal = jnp.triu(jnp.ones((S, S), dtype=bool), k=1)
        scores = jnp.where(causal[None, None], -jnp.inf, scores)
        scores = scores + _alibi_bias(S)[None]
        probs = jax.nn.softmax(scores, axis=-1)
        out = jnp.einsum('bhqk,bhkd->bhqd', probs, v)
        out = out.transpose(0, 2, 1, 3).reshape(B, S, E)
        return out @ Wo.T + bo

    def _L1_ffn_ref(x, gate_w, w1, w2, w3, sw1, sw2, sw3):
        import jax, jax.numpy as jnp
        import numpy as np
        B, S, D = (2, 256, 256)
        E, H, TOP_K = (8, 176, 2)
        SH = 176
        ROUTED_SCALE = 2.5
        b, s, d = x.shape
        xt = x.reshape(b * s, d)
        scores = jax.nn.sigmoid(xt @ gate_w.T)
        top_scores, top_idx = jax.lax.top_k(scores, TOP_K)
        top_scores = top_scores / (jnp.sum(top_scores, axis=-1, keepdims=True) + 1e-20)
        top_scores = top_scores * ROUTED_SCALE
        combine = jnp.sum(jax.nn.one_hot(top_idx, E, dtype=xt.dtype) * top_scores[..., None], axis=1)
        h = jnp.einsum('td,edh->eth', xt, w1)
        u = jnp.einsum('td,edh->eth', xt, w3)
        y = jnp.einsum('eth,ehd->etd', jax.nn.silu(h) * u, w2)
        routed = jnp.einsum('etd,te->td', y, combine)
        shared = jax.nn.silu(xt @ sw1) * (xt @ sw3) @ sw2
        return (routed + shared).reshape(b, s, d)
    x = L0_attn_x
    x = x + 0.5 * _L0_ffn_ref(_layernorm(x, axis=-1), L0_ffn_W1, L0_ffn_W2, L0_ffn_W3)
    x = x + _L0_attn_ref(_layernorm(x, axis=-1), L0_attn_W_in, L0_attn_conv_w, L0_attn_conv_b, L0_attn_W_x, L0_attn_W_dt, L0_attn_b_dt, L0_attn_A_log, L0_attn_Dp, L0_attn_W_out)
    x = x + 0.5 * _L0_ffn_ref(_layernorm(x, axis=-1), L0_ffn_W1, L0_ffn_W2, L0_ffn_W3)
    x = x + 0.5 * _L1_ffn_ref(_layernorm(x, axis=-1), L1_ffn_gate_w, L1_ffn_w1, L1_ffn_w2, L1_ffn_w3, L1_ffn_sw1, L1_ffn_sw2, L1_ffn_sw3)
    x = x + _L1_attn_ref(_layernorm(x, axis=-1), L1_attn_Wq, L1_attn_bq, L1_attn_Wk, L1_attn_bk, L1_attn_Wv, L1_attn_bv, L1_attn_Wo, L1_attn_bo)
    x = x + 0.5 * _L1_ffn_ref(_layernorm(x, axis=-1), L1_ffn_gate_w, L1_ffn_w1, L1_ffn_w2, L1_ffn_w3, L1_ffn_sw1, L1_ffn_sw2, L1_ffn_sw3)
    return x

_drawn_inputs = setup_inputs


def setup_inputs(seed=0):
    import zlib

    import numpy as np

    out = dict(_drawn_inputs(seed))
    spreads = {'L0_attn_Dp': (1.0, 0.6),
     'L1_attn_bq': (0.0, 2.0),
     'L1_attn_bk': (0.0, 2.0),
     'L1_attn_bv': (0.0, 2.0),
     'L1_attn_bo': (0.0, 2.0)}
    factors = {'L0_attn_W_in': 8.0,
     'L0_attn_conv_w': 8.0,
     'L0_attn_conv_b': 8.0,
     'L0_attn_W_x': 8.0,
     'L0_attn_W_dt': 8.0,
     'L0_attn_b_dt': 8.0,
     'L0_attn_A_log': 8.0,
     'L0_attn_W_out': 8.0,
     'L1_ffn_gate_w': 28.632,
     'L1_ffn_w1': 24.888,
     'L1_ffn_w2': 24.576,
     'L1_ffn_w3': 24.616,
     'L1_ffn_sw1': 42.192,
     'L1_ffn_sw2': 41.664,
     'L1_ffn_sw3': 41.952,
     'L1_attn_Wq': 8.0,
     'L1_attn_Wk': 8.0,
     'L1_attn_Wv': 8.0,
     'L1_attn_Wo': 8.0}
    for name, (base, spread) in spreads.items():
        noise = np.random.default_rng([zlib.crc32(name.encode()), seed]).standard_normal(out[name].shape)
        drawn = base * np.exp(spread * noise) if base else spread * noise
        out[name] = jnp.asarray(drawn.astype(out[name].dtype))
    for name, factor in factors.items():
        out[name] = (out[name] * factor).astype(out[name].dtype)
    return out
```

```python
import concourse.bass as bass
from concourse import mybir
from contextlib import ExitStack
import numpy as np

F32 = mybir.dt.float32
BF16 = mybir.dt.bfloat16
ALU = mybir.AluOpType
ACT = mybir.ActivationFunctionType
AX = mybir.AxisListType

P = 128
NB, T, D = 2, 512, 256
TC, DC = T // P, D // P
FH = 1024
FM = FH // P
DI, DS, DTR, DCONV = 512, 16, 128, 4
EC = DI // P
NE, EH = 8, 176
RC = NE * EH // P
MH = (NE + 1) * EH
MM = -(-MH // P)
LAST_ROWS = MH - (MM - 1) * P
MOE_ORDER = list(range(RC, MM)) + list(range(RC))
NH, HD = 16, 16
SLOTS = 6
Q_PART = (0, 0, 1, 1, 0, 2)
K_PART = (0, 1, 0, 1, 2, 0)
POS_ROW = SLOTS * HD
MAX_ROW = POS_ROW + 12
STACK = MAX_ROW + 3
TILE_COLS = [T - P * kc for kc in range(TC)]
TILE_AT = [0, 512, 1024, 512 + TILE_COLS[1]]
PT_COLS = sum(TILE_COLS)
EPS = 1e-5
HEAD = 1
COMB_AT = 768
VEC_ROWS = 3 * (DI // P) + 3 * DC
MOE_LOADS, COL_LOADS = 9, 2
FFN0, MAMBA, FFN1, MOE0, ATTN, MOE1 = range(6)

CF = {"ident": (0, 128), "hadamard": (128, 256), "lower": (256, 320)}
CF_COLS = 320
CB = {"ident": (0, 128), "mask_q": (128, 256), "mask_k": (256, 384), "pick": (384, 416),
      "expert": (416, 416 + RC * P), "zero": (416 + RC * P, 416 + RC * P + 512)}
CB_COLS = 416 + RC * P + 512


def build(nc, x, W_in, conv_w, conv_b, W_x, W_dt, b_dt, A_log, Dp, W_out, W1, W2, W3, Wq, bq, Wk, bk,
          Wv, bv, Wo, bo, gate_w, w1, w2, w3, sw1, sw2, sw3, const_f, const_b, aux_q, aux_k, out):
    ctx = ExitStack()
    with ctx:
        def sb(name, cols, dt=F32):
            return ctx.enter_context(nc.sbuf_tensor(name, [P, cols], dt))

        def sem(name):
            return ctx.enter_context(nc.semaphore(name))

        x_tok = sb("x_tok", NB * TC * D)
        xn_tok = sb("xn_tok", TC * D)
        xnT = sb("xnT", NB * DC * T)
        w1s, w3s = sb("w1s", DC * MH), sb("w3s", DC * MH)
        w2s = sb("w2s", MM * D)
        attn_w = sb("attn_w", 4 * DC * D)
        cf, cb = sb("cf", CF_COLS), sb("cb", CB_COLS, BF16)
        cols = sb("cols", 128)
        stats = sb("stats", 64)
        gated = sb("gated", 2 * T)
        route = sb("route", 1024)
        gateT = sb("gateT", DC * NE)
        sigT = sb("sigT", T)
        combT = sb("combT", T, BF16)
        ones_row = sb("ones_row", P)
        bo_row = sb("bo_row", D)
        R1 = sb("R1", MM * T)
        R2 = sb("R2", 10624)
        R3 = sb("R3", 13568)
        PS = ctx.enter_context(nc.psum_tensor("PS", [P, 8 * 512], F32))

        scratch_q = nc.dram_tensor("scratch_q", (3, 256, T), BF16, kind="Internal").ap()
        scratch_k = nc.dram_tensor("scratch_k", (3, 256, T), BF16, kind="Internal").ap()
        scratch_m = nc.dram_tensor("scratch_m", (3, NH * TC, P), BF16, kind="Internal").ap()

        def bank(i, n=1):
            return PS[:, i * 512:(i + n) * 512]

        def cut(region, at, n, dt=F32):
            words = n if dt == F32 else n // 2
            v = region[:, at:at + words]
            return (v if dt == F32 else v.bitcast(dt)), at + words

        def const_of(t, table, name):
            return t[:, table[name][0]:table[name][1]]

        ident, hadamard, lower = (const_of(cf, CF, n) for n in ("ident", "hadamard", "lower"))
        ident_b, mask_q, mask_k, pick, expert_b, zero_b = (
            const_of(cb, CB, n) for n in ("ident", "mask_q", "mask_k", "pick", "expert", "zero"))
        c_convw = cols[:, 0:16]
        c_convb, c_bdt, c_D = cols[:, 16:20], cols[:, 20:24], cols[:, 24:28]
        c_bq, c_bk, c_bv = cols[:, 28:30], cols[:, 30:32], cols[:, 32:34]
        c_A = cols[:, 64:128]

        hid = R1
        xc, a = cut(R1, 0, EC * T)
        zs, a = cut(R1, a, EC * T)
        delta, a = cut(R1, a, EC * T)
        dtT, a = cut(R1, a, T)
        w2_raw, a = cut(R1, 0, DC * FH)
        w2_mix, a = cut(R1, a, DC * FH)
        w2_raw2, a = cut(R1, a, DC * FH)
        W1T, a = cut(R2, 0, DC * FH)
        W3T, a = cut(R2, a, DC * FH)
        W2T, a = cut(R2, a, FM * D)
        WinT, a = cut(R2, a, DC * 2 * DI)
        WxdT, a = cut(R2, a, EC * DTR)
        WxbT, a = cut(R2, a, EC * 96)
        WdtT, a = cut(R2, a, DI)
        WoutT, a = cut(R2, a, EC * D)
        q_stack, a = cut(R2, 0, NH * T, BF16)
        k_stack, a = cut(R2, a, NH * T, BF16)
        v_tok, a = cut(R2, a, TC * D)
        oT, a = cut(R2, a, DC * T)
        WqT, WkT, WvT, WoT = (attn_w[:, i * DC * D:(i + 1) * DC * D] for i in range(4))
        raw = {}
        a = 0
        for name, n in (("W1", 2048), ("W3", 2048), ("Win", 2048), ("Wx", 512), ("Wxb", 512), ("Wdt", 512),
                        ("Wout", 1024), ("Wq", 512), ("Wk", 512), ("Wv", 512), ("Wo", 512), ("gate", 256), ("vec", 128)):
            raw[name], a = cut(R3, a, n)
        dx, a = cut(R3, 0, EC * T)
        dbx, a = cut(R3, a, 4 * 2 * T)
        hst, a = cut(R3, a, 2 * 2 * T)
        hc, a = cut(R3, a, 4 * 2 * T)
        sp_pos, sp_low = hc[:, 0:EC * T], hc[:, EC * T:2 * EC * T]
        c_bc, a = cut(R3, a, 2 * T)
        bc_stack, a = cut(R3, a, T, BF16)
        bc_rest, bc_hi, bc_mid = hst[:, 0:T], hst[:, T:3 * T // 2].bitcast(BF16), hst[:, 3 * T // 2:2 * T].bitcast(BF16)
        q32, a = cut(R3, 0, DC * T)
        k32, a = cut(R3, a, DC * T)
        v32, a = cut(R3, a, DC * T)
        q_parts, a = cut(R3, a, 3 * DC * T, BF16)
        k_parts, a = cut(R3, a, 3 * DC * T, BF16)
        v_four, a = cut(R3, a, TC * 4 * 32)
        pT, a = cut(R3, a, 2 * PT_COLS)
        o_four, a = cut(R3, a, T)
        o_tok, a = cut(R3, a, TC * D)
        m_all, a = cut(R3, a, NH * TC)
        m_rest, a = cut(R3, a, NH * TC)
        m_parts, a = cut(R3, a, 4 * NH * TC, BF16)
        m_rows, a = cut(R3, a, 2 * P, BF16)
        recip, a = cut(R3, a, 16)

        ld = {n: sem("ld_" + n) for n in ("x", "const", "W1", "W3", "W2", "Win", "Wx", "Wdt", "Wout", "attn",
                                          "cols", "gate", "vec", "moe", "bo", "aux")}
        prep_tr, prep_ev = sem("prep_tr"), [sem("prep_ev0"), sem("prep_ev1")]
        w2_mixed, w2_up, w2_ev, had_up, had_ev = (sem(n) for n in ("w2_mixed", "w2_up", "w2_ev", "had_up", "had_ev"))
        col_ready, a_ready = sem("col_ready"), sem("a_ready")
        var_ready, sd_ready = sem("var_ready"), sem("sd_ready")
        xn_done, xnT_tr, xnT_ev = sem("xn_done"), sem("xnT_tr"), sem("xnT_ev")
        down_done, resid_done = sem("down_done"), sem("resid_done")
        dve_chain = sem("dve_chain")
        stored = sem("stored")

        def stage_sems(stage, names):
            return {n: sem(f"s{stage}_{n}") for n in names}

        S = {}
        for st in (FFN0, FFN1):
            S[st] = stage_sems(st, ("up", "silu", "hid"))
        for st in (MOE0, MOE1):
            S[st] = stage_sems(st, ("up", "silu", "hid", "score", "sig", "sigt", "comb", "combt", "combT", "cb",
                                          "mixed"))
        S[MAMBA] = stage_sems(MAMBA, ("xp", "z", "ini", "conv", "xc", "zs", "dt", "dtT", "bc", "stack", "dl", "abs", "e", "ln", "lo", "sp",
                                      "col0", "B", "C", "cev", "dA", "mul", "scan", "hc", "ys", "yf"))
        S[ATTN] = stage_sems(ATTN, ("qkv", "qkv_ev", "vt", "vtok", "parts", "wrote0", "wrote1", "stacked", "s1", "max", "mparts",
                                    "mt", "mrows", "mwrote", "mstacked", "s2", "p", "v4", "av", "o4", "ot", "otok",
                                    "oT_up", "oT", "rc"))

        HEADED = {"DVE": [resid_done, S[MAMBA]["mul"], S[MAMBA]["scan"], S[ATTN]["max"], S[ATTN]["otok"]]
                  + [S[st]["hid"] for st in (FFN0, FFN1, MOE0, MOE1)],
                  "ACT": [S[MAMBA]["cev"], S[ATTN]["p"], S[ATTN]["o4"]], "POOL": [S[MAMBA]["hc"]],
                  "PE": [S[MAMBA]["ys"], S[ATTN]["av"], S[ATTN]["ot"]]}

        def start_heads(eng, name):
            for h in HEADED[name]:
                eng.sem_inc(h, HEAD)

        def over_batches(eng, body, peeled=False):
            if peeled:
                body(0)
                body(1)
            else:
                with eng.Fori(0, NB) as b:
                    body(b)

        class TensorProgram:
            def __init__(self, pe):
                self.pe = pe

            def prepare(self):
                pe, n = self.pe, 0
                pe.wait_ge(ld["const"], 32)
                for name, groups in PREP:
                    pe.wait_ge(ld[PREP_LOAD[name]], PREP_COUNT[name])
                    for group in groups:
                        if n >= 2:
                            pe.wait_ge(prep_ev[n % 2], n // 2)
                        for at, width, src in group:
                            last = nc.tensor.transpose(bank(n % 2)[0:src.shape[1], at:at + width], src,
                                                       ident[0:width, 0:width])
                        last.then_inc(prep_tr, 1)
                        n += 1
                self.norm_transposes(1, 0)
                for g in range(FM // 2):
                    pe.wait_ge(w2_mixed, 6)
                    if g >= 2:
                        pe.wait_ge(w2_ev, g - 1)
                    for j in range(2):
                        for k in range(DC):
                            src = w2_mix[:, k * FH + (2 * g + j) * P:k * FH + (2 * g + j + 1) * P]
                            last = nc.tensor.transpose(bank(2 + g % 2)[:, (2 * j + k) * P:(2 * j + k + 1) * P], src,
                                                       ident[:, :])
                    last.then_inc(w2_up, 1)
                for g in range(FM // 2):
                    pe.wait_ge(w2_ev, g + 1)
                    if g >= 2:
                        pe.wait_ge(had_ev, g - 1)
                    nc.tensor.matmul(bank(4 + g % 2), hadamard, w2_raw2[:, g * 512:(g + 1) * 512],
                                     start=True, stop=True).then_inc(had_up, 1)

            def norm_transposes(self, k, target):
                pe = self.pe
                pe.wait_ge(xn_done, k)
                for ch in range(DC):
                    pe.wait_ge(xnT_ev, 2 * (k - 1) + ch)
                    for tc in range(TC):
                        last = nc.tensor.transpose(bank(7)[:, tc * P:(tc + 1) * P],
                                                   xn_tok[:, tc * D + ch * P:tc * D + (ch + 1) * P], ident[:, :])
                    last.then_inc(xnT_tr, 1)

            def input_rows(self, b, k):
                return xnT[:, bass.ds(b * DC * T + k * T, T)]

            def down(self, it, chunks, bias=False):
                pe = self.pe
                pe.wait_ge(resid_done, HEAD + it)
                for tc in range(TC):
                    o = bank(5 + tc // 2)[:, (tc % 2) * D:(tc % 2 + 1) * D]
                    for i, (rows, lhs, rhs) in enumerate(chunks):
                        last = nc.tensor.matmul(o, lhs[0:rows, tc * P:(tc + 1) * P], rhs[0:rows, :],
                                                start=(i == 0), stop=(i == len(chunks) - 1 and not bias))
                    if bias:
                        last = nc.tensor.matmul(o, ones_row[0:1, :], bo_row[0:1, :], start=False, stop=True)
                last.then_inc(down_done, 1)

            def ffn(self, st, b):
                pe, s, it = self.pe, S[st], 2 * st + b
                if st == FFN0:
                    pe.wait_ge(had_ev, FM // 2)
                pe.wait_ge(xnT_ev, 2 * it + 2)
                for m in range(FM):
                    pe.wait_ge(s["hid"], HEAD + b * FM + max(m - 1, 0))
                    for w, o in ((W1T, bank(m % 2)), (W3T, bank(2 + m % 2))):
                        for k in range(DC):
                            last = nc.tensor.matmul(o, w[:, k * FH + m * P:k * FH + (m + 1) * P],
                                                    self.input_rows(b, k), start=(k == 0), stop=(k == DC - 1))
                    last.then_inc(s["up"], 1)
                self.norm_transposes(it + 2, 1 - b)
                pe.wait_ge(s["hid"], HEAD + b * FM + FM)
                self.down(it, [(P, hid[:, m * T:(m + 1) * T], W2T[:, m * D:(m + 1) * D]) for m in range(FM)])

            def moe(self, st, b):
                pe, s, it = self.pe, S[st], 2 * st + b
                pe.wait_ge(xnT_ev, 2 * it + 2)
                if st == MOE0:
                    pe.wait_ge(ld["moe"], 16 * MOE_LOADS)
                for k in range(DC):
                    last = nc.tensor.matmul(bank(7)[0:NE, :], gateT[:, k * NE:(k + 1) * NE], self.input_rows(b, k),
                                            start=(k == 0), stop=(k == DC - 1))
                last.then_inc(s["score"], 1)
                for p, m in enumerate(MOE_ORDER):
                    rows = LAST_ROWS if m == MM - 1 else P
                    if p != 1:
                        pe.wait_ge(s["hid"], HEAD + b * MM + max(p - 1, 0))
                    for w, o in ((w1s, bank(p % 2)), (w3s, bank(2 + p % 2))):
                        for k in range(DC):
                            last = nc.tensor.matmul(o[0:rows, :], w[:, k * MH + m * P:k * MH + m * P + rows],
                                                    self.input_rows(b, k), start=(k == 0), stop=(k == DC - 1))
                    last.then_inc(s["up"], 1)
                    if p == 0:
                        pe.wait_ge(s["sig"], b + 1)
                        for tc in range(TC):
                            last = nc.tensor.matmul(bank(7)[:, tc * NE:(tc + 1) * NE],
                                                    sigT[0:NE, tc * P:(tc + 1) * P], ident[0:NE, 0:NE],
                                                    start=True, stop=True)
                        last.then_inc(s["sigt"], 1)
                    if p == 2:
                        pe.wait_ge(s["comb"], b + 1)
                        parts = route[:, COMB_AT:COMB_AT + TC * 3 * NE // 2].bitcast(BF16)
                        for tc in range(TC):
                            last = nc.tensor.transpose(bank(7)[0:3 * NE, :].bitcast(BF16)[:, tc * P:(tc + 1) * P],
                                                       parts[:, tc * 3 * NE:(tc + 1) * 3 * NE], ident_b[:, :])
                        last.then_inc(s["combt"], 1)
                        pe.wait_ge(s["combT"], b + 1)
                    if p >= 2:
                        pe.wait_ge(s["hid"], HEAD + b * MM + p)
                        nc.tensor.matmul(bank(4), expert_b[0:3 * NE, m * P:(m + 1) * P], combT[0:3 * NE, :],
                                         start=True, stop=True).then_inc(s["cb"], 1)
                if st == MOE0 or b == 0:
                    self.norm_transposes(it + 2, 1 - b)
                pe.wait_ge(s["hid"], HEAD + b * MM + MM)
                self.down(it, [(LAST_ROWS if m == MM - 1 else P, hid[:, m * T:(m + 1) * T], w2s[:, m * D:(m + 1) * D])
                               for m in range(MM)])

            def mamba(self, b):
                pe, s, it = self.pe, S[MAMBA], 2 * MAMBA + b
                pe.wait_ge(xnT_ev, 2 * it + 2)
                for c in range(2 * EC):
                    if c >= EC:
                        pe.wait_ge(s["conv"], b * EC + c - EC + 1)
                    for k in range(DC):
                        last = nc.tensor.matmul(bank(c % EC), WinT[:, k * 2 * DI + c * P:k * 2 * DI + (c + 1) * P],
                                                self.input_rows(b, k), start=(k == 0), stop=(k == DC - 1))
                    last.then_inc(s["xp"] if c < EC else s["z"], 1)
                self.norm_transposes(it + 2, 1 - b)
                for k in range(EC):
                    pe.wait_ge(s["xc"], b * EC + k + 1)
                    last = nc.tensor.matmul(bank(4), WxdT[:, k * DTR:(k + 1) * DTR], xc[:, k * T:(k + 1) * T],
                                            start=(k == 0), stop=(k == EC - 1))
                last.then_inc(s["dt"], 1)
                pe.wait_ge(xnT_ev, 2 * it + 4)
                for k in range(EC):
                    last = nc.tensor.matmul(bank(7)[0:96, :], WxbT[:, k * 96:(k + 1) * 96], xc[:, k * T:(k + 1) * T],
                                            start=(k == 0), stop=(k == EC - 1))
                last.then_inc(s["bc"], 1)
                pe.wait_ge(s["dtT"], b + 1)
                for c in range(EC):
                    pe.wait_ge(s["zs"], b * EC + c + 1)
                    nc.tensor.matmul(bank(c), WdtT[:, c * P:(c + 1) * P], dtT, start=True, stop=True)\
                        .then_inc(s["dl"], 1)
                pe.wait_ge(s["stack"], b + 1)
                for half in range(2):
                    g0 = (b * 2 + half) * DS
                    if half == 0:
                        pe.wait_ge(resid_done, HEAD + it)
                    else:
                        pe.wait_ge(s["yf"], b * 2 + 1)
                    for j in range(2):
                        nc.tensor.matmul(bank(5 + j), ident_b[:, :], zero_b[:, :], start=True, stop=False)

                    def broadcast(n, i):
                        pe.wait_ge(s["mul"], HEAD + g0 + n)
                        nc.tensor.matmul(bank(4), pick[0:96, bass.ds(n, 1)].broadcast_to([96, P]),
                                         bc_stack[0:96, :], start=True, stop=True).then_inc(s["B"], 1)
                        pe.wait_ge(s["cev"], HEAD + g0 + n)
                        nc.tensor.matmul(bank(7), pick[0:96, bass.ds(n + DS, 1)].broadcast_to([96, P]),
                                         bc_stack[0:96, :], start=True, stop=True).then_inc(s["C"], 1)

                    def add_state(n, slot, stop=False):
                        pe.wait_ge(s["hc"], HEAD + g0 + n + 1)
                        for j in range(2):
                            last = nc.tensor.matmul(bank(5 + j), ident[:, :],
                                                    hc[:, slot * 2 * T + j * T:slot * 2 * T + (j + 1) * T],
                                                    start=False, stop=stop)
                        last.then_inc(s["ys"], 1)

                    for u in range(4):
                        broadcast(u, u)
                        if u == 3:
                            add_state(0, 0)
                    with pe.Fori(1, 4) as q:
                        for u in range(4):
                            broadcast(q * 4 + u, u)
                            add_state(q * 4 + u - 3, (u + 1) % 4)
                    for n in range(DS - 3, DS):
                        add_state(n, n % 4, stop=(n == DS - 1))
                pe.wait_ge(s["yf"], b * 2 + 2)
                self.down(it, [(P, zs[:, c * T:(c + 1) * T], WoutT[:, c * D:(c + 1) * D]) for c in range(EC)])

            def attention(self, b):
                pe, s, it = self.pe, S[ATTN], 2 * ATTN + b
                pe.wait_ge(xnT_ev, 2 * it + 2)
                for c in range(3 * DC):
                    if c >= 4:
                        pe.wait_ge(s["qkv_ev"], b * 6 + c - 3)
                    w = (WqT, WkT, WvT)[c // DC]
                    for k in range(DC):
                        last = nc.tensor.matmul(bank(c % 4), w[:, k * D + (c % DC) * P:k * D + (c % DC + 1) * P],
                                                self.input_rows(b, k), start=(k == 0), stop=(k == DC - 1))
                    last.then_inc(s["qkv"], 1)
                self.norm_transposes(it + 2, 1 - b)
                for c in range(DC):
                    pe.wait_ge(s["qkv_ev"], b * 6 + 5 + c)
                    if c:
                        pe.wait_ge(s["vtok"], b * DC + c)
                    for tc in range(TC):
                        last = nc.tensor.transpose(bank(4)[:, tc * P:(tc + 1) * P],
                                                   v32[:, c * T + tc * P:c * T + (tc + 1) * P], ident[:, :])
                    last.then_inc(s["vt"], 1)
                with pe.Fori(0, NH // 2) as g:
                    for qc in range(TC):
                        first = 2 * (qc % 2)
                        pe.wait_ge(s["max"], HEAD + b * 32 + g * 4 + qc - 1) if qc else \
                            pe.wait_ge(s["max"], HEAD + b * 32 + g * 4)
                        if qc == 0:
                            pe.wait_ge(ld["aux"], 16 * 2)
                            pe.wait_ge(s["qkv_ev"], b * 6 + 6)
                            pe.wait_ge(s["stacked"], (b + 1) * 16 * 2 * SLOTS)
                        n = (qc + 1) * P
                        for j in range(2):
                            nc.tensor.matmul(bank(first + j)[:, 0:n],
                                             q_stack[0:MAX_ROW, bass.ds((g * 2 + j) * T + qc * P, P)],
                                             k_stack[0:MAX_ROW, bass.ds((g * 2 + j) * T, n)], start=True, stop=False)
                            last = nc.tensor.matmul(bank(first + j)[:, n - P:n], ident_b[:, :], mask_q[:, :],
                                                    start=False, stop=True)
                        last.then_inc(s["s1"], 1)
                pe.wait_ge(s["vtok"], (b + 1) * DC)
                pe.wait_ge(s["mparts"], b + 1)
                for i in range(2):
                    last = nc.tensor.transpose(bank(4).bitcast(BF16)[:, i * P:(i + 1) * P],
                                               m_parts[:, i * P:(i + 1) * P], ident_b[:, :])
                last.then_inc(s["mt"], 1)

                with pe.Fori(0, NH // 4) as hq:
                    def values(j):
                        pe.wait_ge(s["p"], HEAD + b * NH + hq * 4 + j + 1)
                        if j == 0:
                            pe.wait_ge(s["v4"], b * 4 + hq + 1)
                            pe.wait_ge(s["o4"], HEAD + b * 4 + hq)
                        for kc in range(TC):
                            n = TILE_COLS[kc]
                            at = (j % 2) * PT_COLS + TILE_AT[kc]
                            last = nc.tensor.matmul(bank(6)[32 * j:32 * j + 32, kc * P:T],
                                                    v_four[:, (kc * 4 + j) * 32:(kc * 4 + j + 1) * 32],
                                                    pT[:, at:at + n], start=(kc == 0), stop=(kc == TC - 1))
                        last.then_inc(s["av"], 1)

                    for j in range(4):
                        pe.wait_ge(s["p"], HEAD + b * NH + hq * 4 + max(j - 1, 0))
                        if j == 0:
                            pe.wait_ge(s["max"], HEAD + (b + 1) * 32)
                            pe.wait_ge(resid_done, HEAD + it)
                            pe.wait_ge(s["mstacked"], (b + 1) * 16)
                        for kc in range(TC):
                            n = TILE_COLS[kc]
                            o = bank(3 * (j % 2), 3)[:, TILE_AT[kc]:TILE_AT[kc] + n]
                            keys = k_stack[0:STACK, bass.ds((hq * 4 + j) * T + kc * P, P)]
                            nc.tensor.matmul(o, keys, q_stack[0:STACK, bass.ds((hq * 4 + j) * T + kc * P, n)],
                                             start=True, stop=False)
                            last = nc.tensor.matmul(o[:, 0:P], ident_b[:, :], mask_k[:, :], start=False, stop=True)
                        last.then_inc(s["s2"], 1)
                        if j:
                            values(j - 1)
                    values(3)
                    pe.wait_ge(s["o4"], HEAD + b * 4 + hq + 1)
                    pe.wait_ge(s["otok"], HEAD + b * 4 + hq)
                    for tc in range(TC):
                        last = nc.tensor.transpose(bank(7)[:, tc * P:(tc + 1) * P], o_four[:, tc * P:(tc + 1) * P],
                                                   ident[:, :])
                    last.then_inc(s["ot"], 1)
                pe.wait_ge(s["otok"], HEAD + b * 4 + 4)
                for c in range(DC):
                    for tc in range(TC):
                        last = nc.tensor.transpose(bank(c)[:, tc * P:(tc + 1) * P],
                                                   o_tok[:, tc * D + c * P:tc * D + (c + 1) * P], ident[:, :])
                    last.then_inc(s["oT_up"], 1)
                pe.wait_ge(s["oT"], b * DC + DC)
                self.down(it, [(P, oT[:, c * T:(c + 1) * T], WoT[:, c * D:(c + 1) * D]) for c in range(DC)], bias=True)

        class ScalarProgram:
            def __init__(self, act):
                self.act = act

            def prepare(self):
                act, n = self.act, 0
                nc.scalar.preload_act_table(ACT.Sqrt)
                self.norm_sd(1)
                for name, groups in PREP:
                    for group, dst in zip(groups, PREP_DST[name]):
                        if n % 2 == 0:
                            act.wait_ge(prep_tr, n + 1)
                            evacuate(nc.scalar, True, n, dst).then_inc(prep_ev[0], 1)
                        n += 1
                self.norm_evacuate(1, 0)
                self.norm_sd(2)
                for g in range(FM // 2):
                    act.wait_ge(w2_up, g + 1)
                    nc.scalar.activation(w2_raw2[:, g * 512:(g + 1) * 512], bank(2 + g % 2), ACT.Copy)\
                        .then_inc(w2_ev, 1)
                for g in range(FM // 2):
                    act.wait_ge(had_up, g + 1)
                    nc.scalar.activation(W2T[:, g * 512:(g + 1) * 512], bank(4 + g % 2), ACT.Copy).then_inc(had_ev, 1)
                act.wait_ge(ld["cols"], 16 * COL_LOADS)
                nc.scalar.activation(c_A, c_A, ACT.Exp).then_inc(a_ready, 1)
                act.wait_ge(a_ready, 1)
                nc.scalar.mul(c_A, c_A, -1.0).then_inc(a_ready, 1)

            def norm_evacuate(self, k, target):
                for ch in range(DC):
                    self.act.wait_ge(xnT_tr, 2 * (k - 1) + ch + 1)
                    nc.scalar.activation(xnT[:, bass.ds(target * DC * T + ch * T, T)], bank(7), ACT.Copy)\
                        .then_inc(xnT_ev, 1)

            def norm_sd(self, k):
                nc.scalar.preload_act_table(ACT.Sqrt)
                self.act.wait_ge(var_ready, k)
                nc.scalar.activation(stats[:, 36:40], stats[:, 32:36], ACT.Sqrt).then_inc(sd_ready, 1)

            def gate(self, s, b, per_batch, p, slot, first, rows=P):
                act = self.act
                act.wait_ge(s["up"], b * per_batch + p + 1)
                act.wait_ge(s["hid"], HEAD + (b * per_batch if first else b * per_batch + p - 1))
                nc.scalar.activation(gated[0:rows, slot * T:(slot + 1) * T], bank(slot)[0:rows, :], ACT.Silu)\
                    .then_inc(s["silu"], 1)

            def ffn(self, st, b):
                act, s, it = self.act, S[st], 2 * st + b
                nc.scalar.preload_act_table(ACT.Silu)
                for p in range(2):
                    self.gate(s, b, FM, p, p, True)
                with act.Fori(1, FM // 2) as q:
                    for p in range(2):
                        self.gate(s, b, FM, q * 2 + p, p, False)
                self.norm_evacuate(it + 2, 1 - b)
                self.norm_sd(it + 3)

            def moe(self, st, b):
                act, s, it = self.act, S[st], 2 * st + b
                nc.scalar.preload_act_table(ACT.Exp)
                act.wait_ge(s["score"], b + 1)
                nc.scalar.activation(sigT[0:NE, :], bank(7)[0:NE, :], ACT.Exp, scale=-1.0).then_inc(s["sig"], 1)
                nc.scalar.preload_act_table(ACT.Silu)
                for p in range(2):
                    self.gate(s, b, MM, p, p, True, LAST_ROWS if MOE_ORDER[p] == MM - 1 else P)
                act.wait_ge(s["combt"], b + 1)
                nc.scalar.activation(combT[0:3 * NE, :], bank(7)[0:3 * NE, :].bitcast(BF16)[:, 0:T], ACT.Copy)\
                    .then_inc(s["combT"], 1)
                with act.Fori(1, MM // 2) as q:
                    for p in range(2):
                        self.gate(s, b, MM, q * 2 + p, p, False)
                self.gate(s, b, MM, MM - 1, 0, False)
                if st == MOE0 or b == 0:
                    self.norm_evacuate(it + 2, 1 - b)
                if st == MOE0:
                    self.norm_sd(it + 3)

            def mamba(self, b):
                act, s, it = self.act, S[MAMBA], 2 * MAMBA + b
                act.wait_ge(col_ready, 1)
                nc.scalar.preload_act_table(ACT.Silu)

                def chunk(t, c):
                    return t[:, c * T:(c + 1) * T]

                for c in range(EC + 1):
                    if c < EC:
                        act.wait_ge(s["xp"], b * EC + c + 1)
                        nc.scalar.activation(chunk(xc, c), bank(c), ACT.Identity, bias=c_convb[:, c:c + 1],
                                             scale=c_convw[:, c * DCONV + 3:c * DCONV + 4]).then_inc(s["ini"], 1)
                    if c:
                        act.wait_ge(s["conv"], b * EC + c)
                        nc.scalar.activation(chunk(xc, c - 1), chunk(xc, c - 1), ACT.Silu).then_inc(s["xc"], 1)
                for c in range(EC):
                    act.wait_ge(s["z"], b * EC + c + 1)
                    nc.scalar.activation(chunk(zs, c), bank(c), ACT.Silu).then_inc(s["zs"], 1)
                self.norm_evacuate(it + 2, 1 - b)
                act.wait_ge(s["dt"], b + 1)
                nc.scalar.activation(dtT, bank(4), ACT.Copy).then_inc(s["dtT"], 1)
                nc.scalar.preload_act_table_set("natural_log_exp_and_others")
                for h in range(2):
                    for c in (2 * h, 2 * h + 1):
                        act.wait_ge(s["dl"], b * EC + c + 1)
                        nc.scalar.activation(chunk(sp_pos, c), bank(c), ACT.Relu, bias=c_bdt[:, c:c + 1])
                        last = nc.scalar.activation(chunk(delta, c), bank(c), ACT.Abs, bias=c_bdt[:, c:c + 1])
                    last.then_inc(s["abs"], 1)
                    half_of = slice(2 * h * T, 2 * (h + 1) * T)
                    act.wait_ge(s["abs"], b * 2 + h + 1)
                    nc.scalar.activation(delta[:, half_of], delta[:, half_of], ACT.Exp, scale=-1.0).then_inc(s["e"], 1)
                    act.wait_ge(s["e"], b * 2 + h + 1)
                    nc.scalar.activation(dx[:, half_of], delta[:, half_of], ACT.Ln, bias=1.0).then_inc(s["ln"], 1)
                act.wait_ge(s["sp"], (b + 1) * 2)
                act.wait_ge(s["col0"], b + 1)
                act.wait_ge(a_ready, 2)
                for half in range(2):
                    g0 = (b * 2 + half) * DS

                    def step(n, u, first):
                        act.wait_ge(s["scan"], HEAD + (g0 if first else g0 + n - 1))
                        for j in range(2):
                            c = 2 * half + j
                            at = (u % 2) * 2 * T + j * T
                            last = nc.scalar.activation(PS[:, at + 1:at + T], delta[:, c * T + 1:(c + 1) * T], ACT.Exp,
                                                        scale=c_A[:, bass.ds(n + c * DS, 1)])
                        last.then_inc(s["dA"], 1)
                        act.wait_ge(s["C"], g0 + n + 1)
                        act.wait_ge(s["hc"], HEAD + (g0 if first else g0 + n - 1))
                        nc.scalar.activation(c_bc[:, (u % 2) * T:(u % 2 + 1) * T], bank(7), ACT.Copy)\
                            .then_inc(s["cev"], 1)

                    for u in range(4):
                        step(u, u, u < 2)
                    with act.Fori(1, 4) as q:
                        for u in range(4):
                            step(q * 4 + u, u, False)
                self.norm_sd(it + 3)

            def attention(self, b):
                act, s, it = self.act, S[ATTN], 2 * ATTN + b
                for c in range(2, 6):
                    act.wait_ge(s["qkv"], b * 6 + c + 1)
                    dst, bias = (k32, c_bk) if c < 4 else (v32, c_bv)
                    act.wait_ge(s["qkv_ev"], b * 6 + c)
                    nc.scalar.activation(dst[:, (c % 2) * T:(c % 2 + 1) * T], bank(c % 4), ACT.Identity,
                                         bias=bias[:, c % 2:c % 2 + 1]).then_inc(s["qkv_ev"], 1)
                self.norm_evacuate(it + 2, 1 - b)
                for c in range(DC):
                    act.wait_ge(s["vt"], b * DC + c + 1)
                    nc.scalar.activation(v_tok.rearrange("p (t d) -> p t d", t=TC)[:, :, c * P:(c + 1) * P],
                                         bank(4).rearrange("p (t d) -> p t d", t=TC), ACT.Copy).then_inc(s["vtok"], 1)
                act.wait_ge(s["mt"], b + 1)
                nc.scalar.activation(m_rows, bank(4).bitcast(BF16)[:, 0:2 * P], ACT.Copy)\
                    .then_inc(s["mrows"], 1)
                nc.scalar.preload_act_table(ACT.Exp)
                with act.Fori(0, NH // 4) as hq:
                    for j in range(4):
                        act.wait_ge(s["s2"], b * NH + hq * 4 + j + 1)
                        act.wait_ge(s["av"], HEAD + b * NH + hq * 4 + max(j - 1, 0))
                        nc.scalar.activation(pT[:, (j % 2) * PT_COLS:(j % 2 + 1) * PT_COLS],
                                             bank(3 * (j % 2), 3)[:, 0:PT_COLS], ACT.Exp).then_inc(s["p"], 1)
                    act.wait_ge(s["av"], HEAD + b * NH + hq * 4 + 4)
                    act.wait_ge(s["ot"], HEAD + b * 4 + hq)
                    nc.scalar.activation(o_four, bank(6), ACT.Copy).then_inc(s["o4"], 1)
                for c in range(DC):
                    act.wait_ge(s["oT_up"], b * DC + c + 1)
                    nc.scalar.activation(oT[:, c * T:(c + 1) * T], bank(c), ACT.Copy).then_inc(s["oT"], 1)
                self.norm_sd(it + 3)

        class VectorProgram:
            def __init__(self, dve):
                self.dve = dve
                self.base = 0
                self.n = 0
                self.passes = 0

            def link(self, ins):
                self.n += 1
                ins.then_inc(dve_chain, 1)
                self.dve.wait_ge(dve_chain, self.passes + (self.base + self.n))

            def stage(self, body, links, peeled=False):
                def one(b):
                    self.n, self.passes = 0, b * links
                    body(b)
                    assert self.n == links, (self.n, links)
                over_batches(self.dve, one, peeled)
                self.base += NB * links
                self.n, self.passes = 0, 0

            def prepare(self):
                dve, n = self.dve, 0
                dve.wait_ge(ld["x"], 16)
                self.norm(0, 1)
                for name, groups in PREP:
                    for group, dst in zip(groups, PREP_DST[name]):
                        if n % 2 == 1:
                            dve.wait_ge(prep_tr, n + 1)
                            evacuate(nc.vector, False, n, dst).then_inc(prep_ev[1], 1)
                        n += 1
                dve.wait_ge(ld["W2"], 16)
                src, dst = w2_raw, w2_mix
                for i, h in enumerate((1, 2, 4)):
                    def pair(t, side):
                        return t.rearrange("p (g s r) -> p g s r", s=2, r=h * P)[:, :, side, :]
                    for side, op in ((0, ALU.add), (1, ALU.subtract)):
                        last = nc.vector.tensor_tensor(pair(dst, side), pair(src, 0), pair(src, 1), op)
                        last.then_inc(w2_mixed, 1)
                    dve.wait_ge(w2_mixed, 2 * i + 2)
                    src, dst = dst, src
                self.norm(1, 2)
                nc.vector.memset(ones_row[0:1, :], 1.0).then_inc(col_ready, 1)

            def norm(self, b, k, before=None):
                dve = self.dve
                rows = [x_tok[:, bass.ds((b * TC + tc) * D, D)] for tc in range(TC)]
                nc.vector.memset(stats[:, 44:45], 0.0)
                for tc in range(TC):
                    last = nc.vector.bn_stats(stats[:, tc * 6:(tc + 1) * 6], rows[tc])
                self.link(last)
                nc.vector.memset(stats[:, 44:45], 0.0)
                for tc in range(TC):
                    last = nc.vector.bn_aggr(stats[:, 24 + 2 * tc:26 + 2 * tc], stats[:, tc * 6:(tc + 1) * 6])
                self.link(last)
                var = stats[:, 24:32].rearrange("p (t s) -> p t s", s=2)[:, :, 1]
                nc.vector.tensor_scalar_add(stats[:, 32:36], var, EPS).then_inc(var_ready, 1)
                dve.wait_ge(sd_ready, k)
                self.link(nc.vector.reciprocal(stats[:, 40:44], stats[:, 36:40]))
                dve.wait_ge(xnT_tr, 2 * (k - 1))
                for tc in range(TC):
                    last = nc.vector.tensor_scalar(xn_tok[:, tc * D:(tc + 1) * D], rows[tc],
                                                   stats[:, 24 + 2 * tc:25 + 2 * tc], stats[:, 40 + tc:41 + tc],
                                                   ALU.subtract, ALU.mult)
                last.then_inc(xn_done, 1)

            def residual(self, it, b, scale):
                dve = self.dve
                dve.wait_ge(down_done, it + 1)
                for h in range(2):
                    r = x_tok[:, bass.ds((b * TC + 2 * h) * D, 2 * D)]
                    last = nc.vector.scalar_tensor_tensor(r, bank(5 + h), scale, r, ALU.mult, ALU.add)
                last.then_inc(resid_done, 1)
                dve.wait_ge(resid_done, HEAD + it + 1)

            def ffn(self, st, b):
                dve, s, it = self.dve, S[st], 2 * st + b
                with dve.Fori(0, FM // 2) as q:
                    for p in range(2):
                        m = q * 2 + p
                        dve.wait_ge(s["silu"], b * FM + m + 1)
                        nc.vector.tensor_tensor(hid[:, bass.ds(m * T, T)], gated[:, p * T:(p + 1) * T], bank(2 + p),
                                                ALU.mult).then_inc(s["hid"], 1)
                self.residual(it, b, 0.5)
                self.norm(b, it + 3)

            def moe(self, st, b):
                dve, s, it = self.dve, S[st], 2 * st + b

                def shared(p):
                    m = MOE_ORDER[p]
                    rows = LAST_ROWS if m == MM - 1 else P
                    dve.wait_ge(s["silu"], b * MM + p + 1)
                    nc.vector.tensor_tensor(hid[0:rows, m * T:(m + 1) * T], gated[0:rows, p * T:(p + 1) * T],
                                            bank(2 + p)[0:rows, :], ALU.mult).then_inc(s["hid"], 1)

                def routed(p, slot):
                    dve.wait_ge(s["silu"], b * MM + p + 1)
                    product = gated[:, slot * T:(slot + 1) * T]
                    nc.vector.tensor_tensor(product, product, bank(2 + slot), ALU.mult).then_inc(s["mixed"], 1)
                    dve.wait_ge(s["mixed"], b * RC + p - 1)
                    dve.wait_ge(s["cb"], b * RC + p - 1)
                    nc.vector.tensor_tensor(hid[:, bass.ds((p - 2) * T, T)], product, bank(4), ALU.mult)\
                        .then_inc(s["hid"], 1)

                shared(0)
                self.route_weights(s, b)
                shared(1)
                with dve.Fori(1, MM // 2) as q:
                    for p in range(2):
                        routed(q * 2 + p, p)
                routed(MM - 1, 0)
                self.residual(it, b, 0.5)
                if st == MOE0:
                    self.norm(b, it + 3)

            def route_weights(self, s, b):
                dve, v = self.dve, nc.vector
                n = TC * NE
                score, weight = route[:, 0:n], route[:, n:2 * n]
                rank, rest = route[:, 2 * n:3 * n], route[:, 3 * n:4 * n]
                total = route[:, 4 * n:4 * n + TC]
                above = route[:, 256:256 + n * NE]
                equal = route[:, 512:512 + n * NE]

                def grid(t):
                    return t.rearrange("p (t e f) -> p t e f", t=TC, e=NE)

                s3 = score.rearrange("p (t e) -> p t e", t=TC)
                other = s3.unsqueeze(2).broadcast_to([P, TC, NE, NE])
                own = s3.unsqueeze(3).broadcast_to([P, TC, NE, NE])
                dve.wait_ge(s["sigt"], b + 1)
                self.link(v.tensor_scalar_add(score, bank(7)[:, 0:n], 1.0))
                self.link(v.reciprocal(score, score))
                self.link(v.tensor_tensor(grid(above), other, own, ALU.is_gt))
                self.link(v.tensor_tensor(grid(equal), other, own, ALU.is_equal))
                eq = equal.rearrange("p (t f) -> p t f", t=TC)
                self.link(v.tensor_tensor(eq, eq, lower.unsqueeze(1).broadcast_to([P, TC, NE * NE]), ALU.mult))
                self.link(v.tensor_tensor(above, above, equal, ALU.add))
                self.link(v.reduce_sum(rank, above.rearrange("p (a f) -> p a f", f=NE), AX.X))
                self.link(v.scalar_tensor_tensor(weight, rank, 1.5, score, ALU.is_lt, ALU.mult))
                w3d = weight.rearrange("p (t e) -> p t e", t=TC)
                self.link(v.reduce_sum(total, w3d, AX.X))
                self.link(v.tensor_scalar_add(total, total, 1e-20))
                self.link(v.reciprocal(total, total))
                self.link(v.tensor_scalar(total, total, 2.5, None, ALU.mult))
                self.link(v.tensor_tensor(w3d, w3d, total.unsqueeze(2).broadcast_to([P, TC, NE]), ALU.mult))
                parts = route[:, COMB_AT:COMB_AT + n * 3 // 2].bitcast(BF16).rearrange("p (t i e) -> p t i e", t=TC, i=3)
                r3 = rest.rearrange("p (t e) -> p t e", t=TC)
                self.link(v.tensor_copy(parts[:, :, 0, :], w3d))
                self.link(v.tensor_tensor(r3, w3d, parts[:, :, 0, :], ALU.subtract))
                self.link(v.tensor_copy(parts[:, :, 1, :], r3))
                self.link(v.tensor_tensor(r3, r3, parts[:, :, 1, :], ALU.subtract))
                v.tensor_copy(parts[:, :, 2, :], r3).then_inc(s["comb"], 1)

            def mamba(self, b):
                dve, v, s, it = self.dve, nc.vector, S[MAMBA], 2 * MAMBA + b
                for c in range(EC):
                    dve.wait_ge(s["ini"], b * EC + c + 1)
                    for tap in (2, 1, 0):
                        lag = DCONV - 1 - tap
                        o = xc[:, c * T + lag:(c + 1) * T]
                        ins = v.scalar_tensor_tensor(o, bank(c)[:, 0:T - lag],
                                                     c_convw[:, c * DCONV + tap:c * DCONV + tap + 1], o,
                                                     ALU.mult, ALU.add)
                        if tap:
                            self.link(ins)
                        else:
                            ins.then_inc(s["conv"], 1)
                dve.wait_ge(s["bc"], b + 1)
                ps = bank(7)[0:96, :]
                self.link(v.tensor_copy(bc_hi[0:96, :], ps))
                v.tensor_copy(bc_stack[0:32, :], bc_hi[0:32, :])
                self.link(v.tensor_tensor(bc_rest[0:96, :], ps, bc_hi[0:96, :], ALU.subtract))
                self.link(v.tensor_copy(bc_mid[0:96, :], bc_rest[0:96, :]))
                v.tensor_copy(bc_stack[32:64, :], bc_mid[32:64, :])
                self.link(v.tensor_tensor(bc_rest[0:96, :], bc_rest[0:96, :], bc_mid[0:96, :], ALU.subtract))
                v.tensor_copy(bc_stack[64:96, :], bc_rest[64:96, :]).then_inc(s["stack"], 1)
                for h in range(2):
                    r = slice(2 * h * T, 2 * (h + 1) * T)
                    dve.wait_ge(s["e"], b * 2 + h + 1)
                    self.link(v.tensor_scalar_add(sp_low[:, r], delta[:, r], 1.0))
                    self.link(v.scalar_tensor_tensor(sp_low[:, r], sp_low[:, r], 1.0, delta[:, r],
                                                     ALU.subtract, ALU.subtract))
                    v.tensor_tensor(sp_low[:, r], sp_pos[:, r], sp_low[:, r], ALU.subtract).then_inc(s["lo"], 1)
                    dve.wait_ge(s["lo"], b * 2 + h + 1)
                    dve.wait_ge(s["ln"], b * 2 + h + 1)
                    v.tensor_tensor(delta[:, r], sp_low[:, r], dx[:, r], ALU.add).then_inc(s["sp"], 1)
                    dve.wait_ge(s["sp"], b * 2 + h + 1)
                    ins = v.tensor_tensor(dx[:, r], delta[:, r], xc[:, r], ALU.mult)
                self.link(ins)
                v.memset(PS[:, 0:4 * T].rearrange("p (c t) -> p c t", t=T)[:, :, 0:1], 0.0).then_inc(s["col0"], 1)
                for half in range(2):
                    g0 = (b * 2 + half) * DS

                    def times_b(n, u, first=False):
                        dve.wait_ge(s["B"], g0 + n + 1)
                        dve.wait_ge(s["scan"], HEAD + (g0 if first else g0 + n - 2))
                        at = u % 4 * 2 * T
                        v.tensor_tensor(dbx[:, at:at + 2 * T].rearrange("p (c t) -> p c t", c=2),
                                        dx[:, 2 * half * T:2 * (half + 1) * T].rearrange("p (c t) -> p c t", c=2),
                                        bank(4).unsqueeze(1).broadcast_to([P, 2, T]), ALU.mult).then_inc(s["mul"], 1)

                    def scan(n, u, first):
                        at, src = (u % 2) * 2 * T, u * 2 * T
                        dve.wait_ge(s["dA"], g0 + n + 1)
                        dve.wait_ge(s["mul"], HEAD + g0 + n + 1)
                        dve.wait_ge(s["hc"], HEAD + (g0 if first else g0 + n - 1))
                        v.tensor_tensor_scan(hst[:, at:at + 2 * T], PS[:, at:at + 2 * T], dbx[:, src:src + 2 * T], 0.0,
                                             ALU.mult, ALU.add).then_inc(s["scan"], 1)

                    times_b(0, 0, True)
                    for u in range(4):
                        times_b(u + 1, u + 1, u < 2)
                        scan(u, u, u < 2)
                    with dve.Fori(1, 3) as q:
                        for u in range(4):
                            times_b(q * 4 + u + 1, u + 1)
                            scan(q * 4 + u, u, False)
                    for u in range(4):
                        if u < 3:
                            times_b(12 + u + 1, u + 1)
                        scan(12 + u, u, False)
                    dve.wait_ge(s["ys"], HEAD + g0 + DS)
                    for j in range(2):
                        c = 2 * half + j
                        ins = v.scalar_tensor_tensor(xc[:, c * T:(c + 1) * T], xc[:, c * T:(c + 1) * T],
                                                     c_D[:, c:c + 1], bank(5 + j), ALU.mult, ALU.add)
                    self.link(ins)
                    y = slice(2 * half * T, 2 * (half + 1) * T)
                    v.tensor_tensor(zs[:, y], xc[:, y], zs[:, y], ALU.mult).then_inc(s["yf"], 1)
                self.residual(it, b, 1.0)
                self.norm(b, it + 3)

            def attention(self, b):
                dve, v, s, it = self.dve, nc.vector, S[ATTN], 2 * ATTN + b
                n_m = NH * TC
                for c in range(DC):
                    dve.wait_ge(s["qkv"], b * 6 + c + 1)
                    v.tensor_scalar(q32[:, c * T:(c + 1) * T], bank(c), c_bq[:, c:c + 1], HD ** -0.5,
                                    ALU.add, ALU.mult).then_inc(s["qkv_ev"], 1)

                def split(rest, parts, n):
                    for i in range(2):
                        self.link(v.tensor_copy(parts[:, i * n:(i + 1) * n], rest))
                        self.link(v.tensor_tensor(rest, rest, parts[:, i * n:(i + 1) * n], ALU.subtract))
                    return v.tensor_copy(parts[:, 2 * n:3 * n], rest)

                dve.wait_ge(s["qkv_ev"], b * 6 + 2)
                split(q32, q_parts, DC * T).then_inc(s["parts"], 1)
                dve.wait_ge(s["qkv_ev"], b * 6 + 4)
                split(k32, k_parts, DC * T).then_inc(s["parts"], 1)
                v4 = v_four.rearrange("p (k j e) -> p k j e", k=TC, j=4)
                v.memset(m_parts[:, 3 * n_m:4 * n_m], 0.0)
                self.link(v.memset(v_four, 0.0))
                v.memset(v4[:, :, :, HD:HD + 1], 1.0)
                with dve.Fori(0, NH // 2) as g:
                    for qc in range(TC):
                        n = (qc + 1) * P
                        dve.wait_ge(s["s1"], b * 32 + g * 4 + qc + 1)
                        v.reduce_max(m_all.rearrange("p (h c) -> p h c", c=TC)[:, bass.ds(g * 2, 2), qc],
                                     bank(2 * (qc % 2), 2).rearrange("p (j t) -> p j t", j=2)[:, :, 0:n], AX.X)\
                            .then_inc(s["max"], 1)
                dve.wait_ge(s["max"], HEAD + (b + 1) * 32)
                self.link(v.tensor_scalar(m_rest, m_all[:, 0:n_m], -1.0, None, ALU.mult))
                split(m_rest, m_parts, n_m).then_inc(s["mparts"], 1)
                with dve.Fori(0, NH // 4) as hq:
                    dve.wait_ge(s["vtok"], b * DC + DC)
                    dve.wait_ge(s["av"], HEAD + b * NH + hq * 4)
                    v.tensor_copy(v4[:, :, :, 0:HD],
                                  v_tok.rearrange("p (k f) -> p k f", k=TC)[:, :, bass.ds(hq * 4 * HD, 4 * HD)]
                                  .rearrange("p k (j e) -> p k j e", j=4)).then_inc(s["v4"], 1)
                    dve.wait_ge(s["ot"], HEAD + b * 4 + hq + 1)
                    o = bank(7).rearrange("p (a e) -> p a e", e=32)
                    v.reciprocal(recip, o[:, :, HD]).then_inc(s["rc"], 1)
                    dve.wait_ge(s["rc"], b * 4 + hq + 1)
                    v.tensor_tensor(o_tok.rearrange("p (t f) -> p t f", t=TC)[:, :, bass.ds(hq * 4 * HD, 4 * HD)]
                                    .rearrange("p t (j e) -> p t j e", j=4),
                                    bank(7).rearrange("p (t j e) -> p t j e", t=TC, j=4)[:, :, :, 0:HD],
                                    recip.rearrange("p (t j) -> p t j", t=TC).unsqueeze(3)
                                    .broadcast_to([P, TC, 4, HD]), ALU.mult).then_inc(s["otok"], 1)
                self.residual(it, b, 1.0)
                self.norm(b, it + 3)

        def blocks(src, rows, width):
            out_, flat = [], []
            for k in range(width // P):
                for r in range(rows // P):
                    flat.append(src[:, r * width + k * P:r * width + (k + 1) * P])
            for g in range(0, len(flat), 4):
                out_.append([(i * P, P, f) for i, f in enumerate(flat[g:g + 4])])
            return out_

        PREP, PREP_DST = [], {}
        for name, rows, width, dst in (("W1", FH, D, W1T), ("W3", FH, D, W3T), ("Win", 2 * DI, D, WinT),
                                       ("Wx", DTR, DI, WxdT), ("Wdt", DI, DTR, WdtT), ("Wout", D, DI, WoutT),
                                       ("Wq", D, D, WqT), ("Wk", D, D, WkT), ("Wv", D, D, WvT), ("Wo", D, D, WoT)):
            groups = blocks(raw[name], rows, width)
            PREP.append((name, groups))
            PREP_DST[name] = [(P, dst[:, i * 512:(i + 1) * 512], None) for i in range(len(groups))]
        PREP.append(("Wxb", [[(k * 32, 32, raw["Wxb"][0:32, k * P:(k + 1) * P]) for k in range(EC)]]))
        PREP_DST["Wxb"] = [(P, WxbT.rearrange("p (k i c) -> p k i c", k=EC, i=3), "three")]
        PREP.append(("gate", [[(k * NE, NE, raw["gate"][0:NE, k * P:(k + 1) * P]) for k in range(DC)]]))
        PREP_DST["gate"] = [(P, gateT[:, :], DC * NE)]
        PREP.append(("vec", [[(0, VEC_ROWS, raw["vec"][0:VEC_ROWS, :])]]))
        PREP_DST["vec"] = [(P, cols[:, 16:16 + VEC_ROWS], VEC_ROWS)]
        PREP_LOAD = {n: n for n in ("W1", "W3", "Win", "Wdt", "Wout", "gate", "vec")}
        PREP_LOAD.update({"Wx": "Wx", "Wxb": "Wx", "Wq": "attn", "Wk": "attn", "Wv": "attn", "Wo": "attn"})
        PREP_COUNT = {n: 16 for n in PREP_LOAD}
        PREP_COUNT.update({"Wx": 32, "Wxb": 32, "Wq": 64, "Wk": 64, "Wv": 64, "Wo": 64, "vec": 16 * 6})

        def evacuate(eng, is_scalar, n, dst):
            _, d, kind = dst
            src = bank(n % 2)
            if kind == "three":
                src = src[:, 0:EC * 32].rearrange("p (k c) -> p k c", k=EC).unsqueeze(2).broadcast_to([P, EC, 3, 32])
            elif kind:
                src = src[:, 0:kind]
            return eng.activation(d, src, ACT.Copy) if is_scalar else eng.tensor_copy(d, src)


        block = ctx.enter_context(nc.Block())

        @block.sync
        def _(sp):
            def rows_of(w, n=P):
                return w.rearrange("(r p) c -> p r c", p=n)

            def grid(t, r):
                return t.rearrange("p (r c) -> p r c", r=r)

            sp.dma_start(x_tok[:, :].rearrange("p (n d) -> p n d", d=D), x.rearrange("b (t p) d -> p (b t) d", p=P))\
                .then_inc(ld["x"], 16)
            sp.dma_start(cf[:, :], const_f).then_inc(ld["const"], 16)
            sp.dma_start(grid(raw["W1"], FM), rows_of(W1)).then_inc(ld["W1"], 16)
            sp.dma_start(grid(raw["W3"], FM), rows_of(W3)).then_inc(ld["W3"], 16)
            sp.dma_start(grid(w2_raw, DC), rows_of(W2)).then_inc(ld["W2"], 16)
            sp.dma_start(grid(raw["Win"], FM), rows_of(W_in)).then_inc(ld["Win"], 16)
            sp.dma_start(raw["Wx"], W_x[0:DTR, :]).then_inc(ld["Wx"], 16)
            sp.dma_start(raw["Wxb"][0:32, :], W_x[DTR:DTR + 2 * DS, :]).then_inc(ld["Wx"], 16)
            sp.dma_start(grid(raw["Wdt"], EC), rows_of(W_dt)).then_inc(ld["Wdt"], 16)
            sp.dma_start(grid(raw["Wout"], DC), rows_of(W_out)).then_inc(ld["Wout"], 16)
            for name, w in (("Wq", Wq), ("Wk", Wk), ("Wv", Wv), ("Wo", Wo)):
                sp.dma_start(grid(raw[name], DC), rows_of(w)).then_inc(ld["attn"], 16)
            for dst, w, sw in ((w1s, w1, sw1), (w3s, w3, sw3)):
                for k in range(DC):
                    v = dst[:, k * MH:(k + 1) * MH]
                    sp.dma_start(v[:, 0:NE * EH].rearrange("p (e h) -> p e h", e=NE),
                                 w[:, k * P:(k + 1) * P, :].rearrange("e p h -> p e h")).then_inc(ld["moe"], 16)
                sp.dma_start(dst[:, :].rearrange("p (k h) -> p k h", k=DC)[:, :, NE * EH:MH],
                             sw.rearrange("(k p) h -> p k h", p=P)).then_inc(ld["moe"], 16)
            sp.dma_start(w2s[:, 0:RC * D].rearrange("p (m d) -> p m d", m=RC),
                         w2.rearrange("e h d -> (e h) d").rearrange("(m p) d -> p m d", p=P)).then_inc(ld["moe"], 16)
            sp.dma_start(w2s[:, RC * D:(RC + 1) * D], sw2[0:P, :]).then_inc(ld["moe"], 16)
            sp.dma_start(w2s[0:LAST_ROWS, (RC + 1) * D:MM * D], sw2[P:EH, :]).then_inc(ld["moe"], 16)
            sp.wait_ge(down_done, 2 * FFN1 + 2)
            sp.dma_start(k_stack[POS_ROW:STACK, :], aux_k).then_inc(ld["aux"], 16)
            sp.dma_start(q_stack[POS_ROW:MAX_ROW, :], aux_q).then_inc(ld["aux"], 16)

            def attention_moves(b):
                s = S[ATTN]
                for i, (parts, scratch) in enumerate(((q_parts, scratch_q), (k_parts, scratch_k))):
                    sp.wait_ge(s["parts"], b * 2 + i + 1)
                    if i == 0:
                        sp.wait_ge(s["stacked"], b * 16 * 2 * SLOTS)
                    sp.dma_start(scratch.rearrange("i (c p) t -> p i c t", p=P),
                                 parts.rearrange("p (i c t) -> p i c t", i=3, c=DC)).then_inc(s[f"wrote{i}"], 16)
                for i, (stack, scratch, which) in enumerate(((q_stack, scratch_q, Q_PART), (k_stack, scratch_k, K_PART))):
                    sp.wait_ge(s[f"wrote{i}"], (b + 1) * 16)
                    sp.wait_ge(s["s2"], b * NH)
                    sp.wait_ge(down_done, 2 * ATTN + b)
                    for slot, part in enumerate(which):
                        sp.dma_start(stack[slot * HD:(slot + 1) * HD, :].rearrange("p (h t) -> p h t", h=NH),
                                     scratch[part].rearrange("(h d) t -> d h t", d=HD)).then_inc(s["stacked"], 16)
                sp.wait_ge(s["mrows"], b + 1)
                sp.dma_start(scratch_m[0:2].rearrange("i a q -> (i a) q"), m_rows[:, 0:P]).then_inc(s["mwrote"], 16)
                sp.dma_start(scratch_m[2], m_rows[0:NH * TC, P:2 * P]).then_inc(s["mwrote"], 16)
                sp.wait_ge(s["mwrote"], (b + 1) * 32)
                sp.dma_start(q_stack[MAX_ROW:STACK, :], scratch_m.rearrange("i a q -> i (a q)"))\
                    .then_inc(s["mstacked"], 16)

            over_batches(sp, attention_moves, peeled=True)
            for b in range(NB):
                sp.wait_ge(resid_done, HEAD + 2 * MOE1 + b + 1)
                sp.dma_start(out[b].rearrange("(t p) d -> p t d", p=P),
                             x_tok[:, b * TC * D:(b + 1) * TC * D].rearrange("p (t d) -> p t d", d=D))\
                    .then_inc(stored, 16)
            sp.wait_ge(stored, 32)

        @block.gpsimd
        def _(pool):
            def mamba(b):
                s = S[MAMBA]
                for half in range(2):
                    g0 = (b * 2 + half) * DS

                    def step(n, u, first):
                        pool.wait_ge(s["scan"], HEAD + g0 + n + 1)
                        pool.wait_ge(s["cev"], HEAD + g0 + n + 1)
                        pool.wait_ge(s["ys"], HEAD + (g0 if first else g0 + n - 3))
                        nc.gpsimd.tensor_tensor(
                            hc[:, u * 2 * T:(u + 1) * 2 * T].rearrange("p (c t) -> p c t", c=2),
                            hst[:, (u % 2) * 2 * T:(u % 2 + 1) * 2 * T].rearrange("p (c t) -> p c t", c=2),
                            c_bc[:, (u % 2) * T:(u % 2 + 1) * T].unsqueeze(1).broadcast_to([P, 2, T]),
                            ALU.mult).then_inc(s["hc"], 1)

                    for u in range(4):
                        step(u, u, True)
                    with pool.Fori(1, 4) as q:
                        for u in range(4):
                            step(q * 4 + u, u, False)

            start_heads(pool, "POOL")
            over_batches(pool, mamba)

        @block.scalar
        def _(act):
            act.dma_start(cb[:, :], const_b).then_inc(ld["const"], 16)
            act.dma_start(raw["gate"][0:NE, :], gate_w).then_inc(ld["gate"], 16)
            act.dma_start(bo_row[0:1, :], bo.rearrange("(a n) -> a n", a=1)).then_inc(ld["bo"], 16)
            at = 0
            for v in (conv_b, b_dt, Dp, bq, bk, bv):
                n = v.shape[0] // P
                act.dma_start(raw["vec"][at:at + n, :], v.rearrange("(c p) -> c p", p=P)).then_inc(ld["vec"], 16)
                at += n
            act.dma_start(c_convw.rearrange("p (c k) -> p c k", c=EC), conv_w.rearrange("(c p) k -> p c k", p=P))\
                .then_inc(ld["cols"], 16)
            act.dma_start(c_A.rearrange("p (c s) -> p c s", c=EC), A_log.rearrange("(c p) s -> p c s", p=P))\
                .then_inc(ld["cols"], 16)
            start_heads(act, "ACT")
            prog = ScalarProgram(act)
            prog.prepare()
            over_batches(act, lambda b: prog.ffn(FFN0, b))
            over_batches(act, prog.mamba)
            over_batches(act, lambda b: prog.ffn(FFN1, b))
            over_batches(act, lambda b: prog.moe(MOE0, b))
            over_batches(act, prog.attention)
            over_batches(act, lambda b: prog.moe(MOE1, b), peeled=True)

        @block.vector
        def _(dve):
            start_heads(dve, "DVE")
            prog = VectorProgram(dve)
            prog.prepare()
            prog.base = prog.n
            prog.stage(lambda b: prog.ffn(FFN0, b), 3)
            prog.stage(prog.mamba, 22)
            prog.stage(lambda b: prog.ffn(FFN1, b), 3)
            prog.stage(lambda b: prog.moe(MOE0, b), 20)
            prog.stage(prog.attention, 17)
            prog.stage(lambda b: prog.moe(MOE1, b), 17, peeled=True)

        @block.tensor
        def _(pe):
            start_heads(pe, "PE")
            prog = TensorProgram(pe)
            prog.prepare()
            over_batches(pe, lambda b: prog.ffn(FFN0, b))
            over_batches(pe, prog.mamba)
            over_batches(pe, lambda b: prog.ffn(FFN1, b))
            over_batches(pe, lambda b: prog.moe(MOE0, b))
            pe.wait_ge(ld["bo"], 16)
            pe.wait_ge(col_ready, 1)
            over_batches(pe, prog.attention)
            over_batches(pe, lambda b: prog.moe(MOE1, b), peeled=True)


_INS = ['L0_attn_x', 'L0_attn_W_in', 'L0_attn_conv_w', 'L0_attn_conv_b', 'L0_attn_W_x', 'L0_attn_W_dt',
        'L0_attn_b_dt', 'L0_attn_A_log', 'L0_attn_Dp', 'L0_attn_W_out', 'L0_ffn_W1', 'L0_ffn_W2', 'L0_ffn_W3',
        'L1_attn_Wq', 'L1_attn_bq', 'L1_attn_Wk', 'L1_attn_bk', 'L1_attn_Wv', 'L1_attn_bv', 'L1_attn_Wo',
        'L1_attn_bo', 'L1_ffn_gate_w', 'L1_ffn_w1', 'L1_ffn_w2', 'L1_ffn_w3', 'L1_ffn_sw1', 'L1_ffn_sw2',
        'L1_ffn_sw3']


def _constants():
    def bf16(v):
        return (np.ascontiguousarray(v, dtype=np.float32).view(np.uint32) >> 16).astype(np.uint16)

    def parts(v):
        res, rest = [], np.asarray(v, np.float32)
        for _ in range(3):
            hi = (rest.view(np.uint32) & 0xFFFF0000).view(np.float32)
            res.append(hi)
            rest = (rest - hi).astype(np.float32)
        return res

    f = np.zeros((P, CF_COLS), np.float32)
    i = np.arange(P)
    f[:, 0:128] = np.eye(P)
    bits = i[:, None] & i[None, :]
    parity = sum((bits >> s) & 1 for s in range(7)) % 2
    f[:, 128:256] = (1 - 2 * parity) / 32.0
    e = np.arange(NE)
    f[:, 256:320] = (e[None, :] < e[:, None]).reshape(1, -1)

    c = np.zeros((P, CB_COLS), np.float32)
    c[:, 0:128] = np.eye(P)
    c[:, 128:256] = np.where(i[None, :] > i[:, None], -2.0 ** 100, 0)
    c[:, 256:384] = np.where(i[:, None] > i[None, :], -2.0 ** 100, 0)
    for r in range(96):
        c[r, 384 + r % 32] = 1
    for r in range(RC * P):
        for part in range(3):
            c[part * NE + r // EH, CB["expert"][0] + r] = 1

    start = 2.0 ** (-2.0 ** (-(np.log2(NH) - 3)))
    slope = parts(np.array([start * start ** h for h in range(NH)], np.float32))
    pos = np.arange(T)
    halves = [(pos // P * P).astype(np.float32), (pos % P).astype(np.float32)]
    aux_q, aux_k = np.zeros((12, NH, T), np.float32), np.zeros((15, NH, T), np.float32)
    r = 0
    for sp in slope:
        for hv in halves:
            aux_q[r], aux_k[r] = sp[:, None], hv[None, :]
            aux_q[r + 6], aux_k[r + 6] = -hv[None, :], sp[:, None]
            r += 1
    aux_k[12:15] = 1
    return {"const_f": f, "const_b": bf16(c), "aux_q": bf16(aux_q.reshape(12, -1)),
            "aux_k": bf16(aux_k.reshape(15, -1))}


def kernel(**inputs):
    import concourse.bacc as _bacc
    from concourse.bass_utils import run_bass_kernel_spmd as _run

    nc = _bacc.Bacc("TRN2", target_bir_lowering=False, num_devices=1)
    arrays, args = {}, []
    for name in _INS:
        a = np.ascontiguousarray(inputs[name])
        arrays[f"in_{name}_dram"] = a
        args.append(nc.dram_tensor(f"in_{name}_dram", a.shape, mybir.dt.from_np(a.dtype), kind="ExternalInput").ap())
    for name, a in _constants().items():
        arrays[name] = a
        ap = nc.dram_tensor(name, a.shape, mybir.dt.from_np(a.dtype), kind="ExternalInput").ap()
        args.append(ap if a.dtype == np.float32 else ap.bitcast(BF16))
    out = nc.dram_tensor("out_dram", (NB, T, D), F32, kind="ExternalOutput").ap()
    build(nc, *args, out)
    r = _run(nc, [arrays], core_ids=[0])
    return r.results[0]["out_dram"]
```

```python
import concourse.bass as bass
from concourse import mybir
from contextlib import ExitStack
import numpy as np

F32 = mybir.dt.float32
BF16 = mybir.dt.bfloat16
F32R = mybir.dt.float32r
ALU = mybir.AluOpType
ACT = mybir.ActivationFunctionType
AX = mybir.AxisListType

P = 128
NB, T, D = 2, 512, 256
TC, DC = T // P, D // P
FH = 1024
FM = FH // P
DI, DS, DTR, DCONV = 512, 16, 128, 4
EC = DI // P
NE, EH = 8, 176
RC = NE * EH // P
MH = (NE + 1) * EH
MM = -(-MH // P)
LAST_ROWS = MH - (MM - 1) * P
MOE_ORDER = list(range(RC, MM)) + list(range(RC))
NH, HD = 16, 16
SLOTS = 6
Q_RUNS = ((0, 3), (1, 2), (2, 1))
POS_ROW = SLOTS * HD
MAX_ROW = POS_ROW + 12
STACK = MAX_ROW + 3
TILE_COLS = [T - P * kc for kc in range(TC)]
TILE_AT = [0, 512, 1024, 512 + TILE_COLS[1]]
PT_COLS = sum(TILE_COLS)
SOFTPLUS_DVE, SOFTPLUS_POOL = (0, 1), (2, 3)
SOFTPLUS_ORDER = (0, 2, 1, 3)
SOFTPLUS_RANK = tuple(SOFTPLUS_ORDER.index(c) for c in range(EC))
MAX_BANKS = (0, 7)
SUM_BANKS = ((5, 6), (4, 7))
RING = 4
EPS = 1e-5
HEAD = 4
HALVES = 2
HH = NH // HALVES
COMB_AT = 768
VEC_ROWS = 3 * (DI // P) + 3 * DC
MOE_LOADS, COL_LOADS = 9, 2
FFN0, MAMBA, FFN1, MOE0, ATTN, MOE1 = range(6)

FFN_WORDS = 6 * DC * FH
MAMBA_W_AT = FFN_WORDS
MAMBA_W_WORDS = 2 * DC * 2 * DI + EC * DTR + DI + EC * D
ATTN_W_AT = MAMBA_W_AT + MAMBA_W_WORDS
WORK_AT = ATTN_W_AT + 7 * DC * D
MOE_RAW_WORDS = 2 * DC * MH + MM * D
SHARED = WORK_AT + 9 * EC * T
MOE_RAW_AT = SHARED - MOE_RAW_WORDS

CF = {"ident": (0, 128), "hadamard": (128, 256), "lower": (256, 320)}
CF_COLS = 320
CB = {"ident": (0, 128), "mask_q": (128, 256), "mask_k": (256, 384), "pick": (384, 416),
      "expert": (416, 416 + RC * P), "zero": (416 + RC * P, 416 + RC * P + 512)}
CB_COLS = 416 + RC * P + 512


def build(nc, x, W_in, conv_w, conv_b, W_x, W_dt, b_dt, A_log, Dp, W_out, W1, W2, W3, Wq, bq, Wk, bk,
          Wv, bv, Wo, bo, gate_w, w1, w2, w3, sw1, sw2, sw3, const_f, const_b, aux_q, aux_k, out):
    ctx = ExitStack()
    with ctx:
        def sb(name, cols, dt=F32):
            return ctx.enter_context(nc.sbuf_tensor(name, [P, cols], dt))

        def sem(name):
            return ctx.enter_context(nc.semaphore(name))

        x_tok = sb("x_tok", NB * TC * D)
        xn_tok = sb("xn_tok", TC * D)
        xnT = sb("xnT", 2 * NB * DC * T, F32R)
        xnT_hi, xnT_lo = xnT[:, 0:NB * DC * T], xnT[:, NB * DC * T:]
        cf, cb = sb("cf", CF_COLS), sb("cb", CB_COLS, BF16)
        cols = sb("cols", 128)
        stats = sb("stats", 64)
        gated = sb("gated", 2 * T)
        route = sb("route", 1024)
        gateT = sb("gateT", 2 * DC * NE, F32R)
        sigT = sb("sigT", T)
        combT = sb("combT", T, BF16)
        ones_row = sb("ones_row", P)
        bo_row = sb("bo_row", D)
        with nc.sbuf_tensor("shared", [P, SHARED], F32) as shared:
            pass
        with nc.sbuf_tensor("below_moe_raw", [P, MOE_RAW_AT], F32), \
                nc.sbuf_tensor("moe_raw", [P, MOE_RAW_WORDS], F32) as moe_raw:
            pass
        weights_r = sb("weights_r", WORK_AT, F32R)
        work_r = sb("work_r", SHARED - WORK_AT, F32R)
        PS = ctx.enter_context(nc.psum_tensor("PS", [P, 8 * 512], F32))

        scratch_q = nc.dram_tensor("scratch_q", (DC, 3, HD, HH, T), BF16, kind="Internal").ap()
        scratch_k = nc.dram_tensor("scratch_k", (DC, 3, HD, HH, T), BF16, kind="Internal").ap()
        scratch_m = nc.dram_tensor("scratch_m", (HALVES, 3 * HH * TC, P), BF16, kind="Internal").ap()

        def bank(i, n=1):
            return PS[:, i * 512:(i + n) * 512]

        def cut(region, at, n, dt=F32):
            words = n // 2 if dt == BF16 else n
            v = region[:, at:at + words]
            return (v.bitcast(dt) if dt == BF16 else v), at + words

        def halves(at, n):
            t, off = (weights_r, 0) if at < WORK_AT else (work_r, WORK_AT)
            return (t[:, at - off:at - off + n], t[:, at - off + n:at - off + 2 * n]), at + 2 * n

        def const_of(t, table, name):
            return t[:, table[name][0]:table[name][1]]

        ident, hadamard, lower = (const_of(cf, CF, n) for n in ("ident", "hadamard", "lower"))
        ident_b, mask_q, mask_k, pick, expert_b, zero_b = (
            const_of(cb, CB, n) for n in ("ident", "mask_q", "mask_k", "pick", "expert", "zero"))
        c_convw = cols[:, 0:16]
        c_convb, c_bdt, c_D = cols[:, 16:20], cols[:, 20:24], cols[:, 24:28]
        c_bq, c_bk, c_bv = cols[:, 28:30], cols[:, 30:32], cols[:, 32:34]
        minus_one = cols[:, 48:49]
        c_A = cols[:, 64:128]

        W2T, a = halves(0, FM * D)
        W1T, a = halves(a, DC * FH)
        W3T, a = halves(a, DC * FH)
        WinT, a = halves(a, DC * 2 * DI)
        WxdT, a = cut(shared, a, EC * DTR)
        WdtT, a = cut(shared, a, DI)
        WoutT, a = cut(shared, a, EC * D)
        WxbT = sigT[:, 0:EC * 96]
        WqT, a = halves(a, DC * D)
        WkT, a = halves(a, DC * D)
        WvT, a = halves(a, DC * D)
        WoT, a = cut(shared, a, DC * D)
        ring = [halves(WORK_AT + i * 2 * T, T)[0] for i in range(RING)]
        w1s, a = cut(moe_raw, 0, DC * MH)
        w3s, a = cut(moe_raw, a, DC * MH)
        w2s, a = cut(moe_raw, a, MM * D)
        w2_hi, a = cut(weights_r, 0, MM * D)
        w1h, a = halves(a, DC * MH)
        w3h, a = halves(a, DC * MH)
        assert a <= ATTN_W_AT
        assert all(MM * D + m * P >= 2 * FM * D for m in MOE_ORDER[:2])
        w2_lo, a = cut(work_r, RING * 2 * T, MM * D)
        moe_end = WORK_AT + a
        raw = {}
        a = WORK_AT
        for name, n in (("W1", 2048), ("W3", 2048), ("Win", 2048), ("Wx", 512), ("Wxb", 512), ("Wdt", 512),
                        ("Wout", 1024), ("Wq", 512), ("Wk", 512), ("Wv", 512), ("Wo", 512),
                        ("gate", 256), ("vec", 128)):
            raw[name], a = cut(shared, a, n)
        w2_raw, a = cut(shared, a, DC * FH)
        w2_mix, a = cut(shared, a, DC * FH)
        w2_raw2, a = cut(shared, a, DC * FH)
        xc, a = cut(shared, WORK_AT, EC * T)
        zs, a = cut(shared, a, EC * T)
        delta, a = cut(shared, a, EC * T)
        dx, a = cut(shared, a, EC * T)
        dbx, a = cut(shared, a, 4 * 2 * T)
        hst, a = cut(shared, a, 2 * 2 * T)
        hc, a = cut(shared, a, 4 * 2 * T)
        assert a == SHARED
        dtT = dbx[:, 7 * T:8 * T]
        sp_pos = [hc[:, c * T:(c + 1) * T] for c in range(EC)]
        sp_low = [hc[:, (EC + c) * T:(EC + c + 1) * T] for c in range(EC)]
        c_bc, bc_stack = xn_tok, combT
        bc_rest = hst[:, 0:T]
        bc_hi, bc_mid = hst[:, T:3 * T // 2].bitcast(BF16), hst[:, 3 * T // 2:2 * T].bitcast(BF16)
        decay = (gated[:, :], route[:, :])
        q_stack, a = cut(shared, 0, NH * T, BF16)
        k_stack, a = cut(shared, a, NH * T, BF16)
        v_tok, a = cut(shared, a, TC * D)
        q32, a = cut(shared, a, DC * T)
        k32, a = cut(shared, a, DC * T)
        v32, a = cut(shared, a, DC * T)
        q_parts, a = cut(shared, a, 3 * DC * T, BF16)
        k_parts, a = cut(shared, a, 3 * DC * T, BF16)
        m_all, a = cut(shared, a, NH * TC)
        m_rest, a = cut(shared, a, NH * TC)
        m_parts, a = cut(shared, a, 3 * NH * TC, BF16)
        m_rows, a = cut(shared, a, HALVES * P, BF16)
        w2_end = 4 * DC * MH + MM * D
        o_four, a = cut(shared, max(a, w2_end), T)
        o_tok, a = cut(shared, a, TC * D)
        recip, a = cut(shared, a, 16)
        assert a <= ATTN_W_AT
        v_four, a = cut(shared, WORK_AT, TC * 4 * 32)
        pT, a = cut(shared, a, 2 * PT_COLS)
        assert a <= moe_end
        oT, a = cut(shared, moe_end, DC * T)
        assert a <= MOE_RAW_AT

        def part_of(parts, c, i):
            return parts[:, (c * 3 + i) * T:(c * 3 + i + 1) * T]

        ld = {n: sem("ld_" + n) for n in ("x0", "x1", "const", "W1", "W3", "W2", "Win", "Wx", "Wdt", "Wout", "attn",
                                          "cols", "gate", "vec", "moe", "bo", "aux")}
        prep_tr, prep_ev, prep_low = sem("prep_tr"), sem("prep_ev"), sem("prep_low")
        rest_tr, rest_ev, rest_low = sem("rest_tr"), sem("rest_ev"), sem("rest_low")
        w2_mixed, w2_up, w2_ev, had_up, had_ev = (sem(n) for n in ("w2_mixed", "w2_up", "w2_ev", "had_up", "had_ev"))
        had_hi, moe_hi, moe_split = sem("had_hi"), sem("moe_hi"), sem("moe_split")
        col_ready, a_ready = sem("col_ready"), sem("a_ready")
        var_ready, sd_ready = sem("var_ready"), sem("sd_ready")
        xn_done, xnT_tr = sem("xn_done"), sem("xnT_tr")
        xnT_high, xnT_ev = sem("xnT_high"), sem("xnT_ev")
        down_done, resid_done = sem("down_done"), sem("resid_done")
        dve_chain = sem("dve_chain")
        stored = sem("stored")

        def stage_sems(stage, names):
            return {n: sem(f"s{stage}_{n}") for n in names}

        S = {}
        for st in (FFN0, FFN1):
            S[st] = stage_sems(st, ("up", "silu", "prod", "high", "hid", "used"))
        for st in (MOE0, MOE1):
            S[st] = stage_sems(st, ("up", "silu", "prod", "high", "hid", "used", "score", "sig", "sigt",
                                    "comb", "combt", "combT", "cb", "mixed"))
        S[MAMBA] = stage_sems(MAMBA, ("xp", "z", "ini", "tap", "xc", "zs", "dt", "dtT", "bc", "stack", "dl", "abs",
                                      "e", "ln", "u", "sp", "dx", "dx_p", "col0", "B", "C", "cev", "dA", "mul",
                                      "scan", "hc", "ys", "yf"))
        TAPS = sorted(((c, DCONV - 2 - i) for c in range(EC) for i in range(DCONV - 1)),
                      key=lambda ct: (2 * ct[0] + (DCONV - 2 - ct[1]) * 1.5, ct[0]))

        def tap_at(b, c, tap):
            return b * len(TAPS) + (TAPS.index((c, tap)) + 1)

        S[ATTN] = stage_sems(ATTN, ("qkv", "cast", "rest", "v_ev", "vt", "vtok", "wroteq0", "wroteq1", "wrotek0",
                                    "wrotek1", "stacked0", "stacked1", "stacked2", "stacked3", "s1", "max",
                                    "mparts", "mt", "mrows", "mwrote0", "mwrote1", "mstacked0", "mstacked1",
                                    "s2", "p", "v4", "av", "o4", "ot", "otok", "oT_up", "oT", "rc"))
        CAST = {n: i + 1 for i, n in enumerate(("k32", "k_hi", "q_hi", "k_mid", "q_mid", "k_lo", "q_lo"))}
        REST = {n: i + 1 for i, n in enumerate(("q32", "k_1", "q_1", "k_2", "q_2"))}

        def cast_at(b, c, name):
            return b * (DC * len(CAST)) + (c * len(CAST) + CAST[name])

        def rest_at(b, c, name):
            return b * (DC * len(REST)) + (c * len(REST) + REST[name])

        HEADED = {"DVE": [resid_done, S[MAMBA]["mul"], S[MAMBA]["scan"], S[ATTN]["max"], S[ATTN]["otok"]]
                  + [S[st][n] for st in (FFN0, FFN1, MOE0, MOE1) for n in ("hid", "prod")],
                  "ACT": [S[MAMBA]["cev"], S[ATTN]["p"], S[ATTN]["o4"]], "POOL": [S[MAMBA]["hc"]],
                  "PE": [S[MAMBA]["ys"], S[ATTN]["av"], S[ATTN]["ot"]]
                  + [S[st]["used"] for st in (FFN0, FFN1, MOE0, MOE1)]}

        def start_heads(eng, name):
            for h in HEADED[name]:
                eng.sem_inc(h, HEAD)

        def over_batches(eng, body, peeled=False):
            if peeled:
                body(0)
                body(1)
            else:
                with eng.Fori(0, NB) as b:
                    body(b)

        def add_softplus(eng, c, link, wait_for_log):
            pos, low = sp_pos[c], sp_low[c]
            dt_, x_, o = (t[:, c * T:(c + 1) * T] for t in (delta, xc, dx))
            link(eng.tensor_tensor(low, low, dt_, ALU.subtract))
            link(eng.tensor_tensor(low, pos, low, ALU.subtract))
            wait_for_log()
            link(eng.tensor_tensor(dt_, low, o, ALU.add))
            return eng.tensor_tensor(o, dt_, x_, ALU.mult)

        class TensorProgram:
            def __init__(self, pe):
                self.pe = pe

            def prepare(self):
                pe = self.pe
                pe.wait_ge(ld["const"], 32)
                for n, (name, group, dst) in enumerate(PREP_FIRST):
                    pe.wait_ge(ld[PREP_LOAD[name]], PREP_COUNT[name])
                    if n >= 4:
                        pe.wait_ge(prep_ev, n - 3)
                        pe.wait_ge(prep_low, n - 3)
                    self.transpose_group(bank(n % 4), group).then_inc(prep_tr, 1)
                self.norm_transposes(1)
                pe.wait_ge(prep_ev, len(PREP_FIRST))
                pe.wait_ge(prep_low, len(PREP_FIRST))

            def transpose_group(self, o, group):
                for at, width, src in group:
                    last = nc.tensor.transpose(o[0:src.shape[1], at:at + width], src, ident[0:width, 0:width])
                return last

            def prepare_w2(self):
                pe = self.pe
                pe.wait_ge(w2_mixed, 6)
                pe.wait_ge(xnT_ev, 2)
                for g in range(FM // 2):
                    if g >= 2:
                        pe.wait_ge(w2_ev, g - 1)
                    for j in range(2):
                        for k in range(DC):
                            src = w2_mix[:, k * FH + (2 * g + j) * P:k * FH + (2 * g + j + 1) * P]
                            last = nc.tensor.transpose(side_bank(g)[:, (2 * j + k) * P:(2 * j + k + 1) * P], src,
                                                       ident[:, :])
                    last.then_inc(w2_up, 1)
                for g in range(FM // 2):
                    pe.wait_ge(w2_ev, g + 1 if g else 3)
                    if g == 1:
                        pe.wait_ge(w2_ev, 4)
                    if g >= 2:
                        pe.wait_ge(had_ev, g - 1)
                    nc.tensor.matmul(side_bank(g), hadamard, w2_raw2[:, g * 512:(g + 1) * 512],
                                     start=True, stop=True).then_inc(had_up, 1)

            def prepare_rest(self, m, i):
                pe = self.pe
                for n in rest_groups(m, i):
                    name, group, _ = PREP_REST[n]
                    pe.wait_ge(ld[PREP_LOAD[name]], PREP_COUNT[name])
                    if n < 2:
                        pe.wait_ge(had_ev, FM // 2)
                    else:
                        pe.wait_ge(rest_ev, n - 1)
                        pe.wait_ge(rest_low, REST_LOWS[n - 1])
                    self.transpose_group(side_bank(n), group).then_inc(rest_tr, 1)

            def product(self, o, lhs, rhs, start, stop):
                for i, (l, r) in enumerate(((1, 0), (0, 1), (0, 0))):
                    last = nc.tensor.matmul(o, lhs[l], rhs[r], start=(start and i == 0), stop=(stop and i == 2))
                return last

            def norm_transpose(self, k, ch, at=7):
                pe = self.pe
                pe.wait_ge(xn_done, k)
                if at == 7:
                    pe.wait_ge(xnT_ev, 2 * (k - 1) + ch)
                for tc in range(TC):
                    last = nc.tensor.transpose(bank(at)[:, tc * P:(tc + 1) * P],
                                               xn_tok[:, tc * D + ch * P:tc * D + (ch + 1) * P], ident[:, :])
                last.then_inc(xnT_tr, 1)

            def norm_transposes(self, k):
                for ch in range(DC):
                    self.norm_transpose(k, ch)

            def input_product(self, o, w, at, rows, stride, b):
                for k in range(DC):
                    cols_ = slice(k * stride + at, k * stride + at + rows)
                    x_ = bass.ds(b * DC * T + k * T, T)
                    last = self.product(o, (w[0][:, cols_], w[1][:, cols_]), (xnT_hi[:, x_], xnT_lo[:, x_]),
                                        k == 0, k == DC - 1)
                return last

            def down(self, it, chunks, bias=False):
                pe = self.pe
                pe.wait_ge(resid_done, HEAD + it)
                for tc in range(TC):
                    o = bank(5 + tc // 2)[:, (tc % 2) * D:(tc % 2 + 1) * D]
                    for i, (rows, lhs, rhs) in enumerate(chunks):
                        last = nc.tensor.matmul(o, lhs[0:rows, tc * P:(tc + 1) * P], rhs[0:rows, :],
                                                start=(i == 0), stop=(i == len(chunks) - 1 and not bias))
                    if bias:
                        last = nc.tensor.matmul(o, ones_row[0:1, :], bo_row[0:1, :], start=False, stop=True)
                last.then_inc(down_done, 1)

            def open_output(self, it):
                self.pe.wait_ge(resid_done, HEAD + it)
                for j in range(2):
                    nc.tensor.matmul(bank(5 + j), ident_b[:, :], zero_b[:, :], start=True, stop=False)

            def down_chunk(self, s, b, count, p, rows, w2, at):
                self.pe.wait_ge(s["hid"], HEAD + b * count + p + 1)
                hi, lo = ring[p % RING]
                for tc in range(TC):
                    t = slice(tc * P, (tc + 1) * P)
                    last = self.product(bank(5 + tc // 2)[:, (tc % 2) * D:(tc % 2 + 1) * D],
                                        (hi[0:rows, t], lo[0:rows, t]),
                                        (w2[0][0:rows, at:at + D], w2[1][0:rows, at:at + D]),
                                        False, p == count - 1 and tc % 2 == 1)
                last.then_inc(s["used"] if p < count - 1 else down_done, 1)

            def ffn(self, st, b):
                pe, s, it = self.pe, S[st], 2 * st + b
                preparing = st == FFN0 and b == 0
                pe.wait_ge(xnT_ev, 2 * it + 2)
                for m in range(FM + 2):
                    if m < FM:
                        pe.wait_ge(s["prod"], HEAD + b * FM + max(m - 1, 0))
                        self.input_product(bank(m % 2), W1T, m * P, P, FH, b)
                        if preparing:
                            self.prepare_rest(m, 0)
                        self.input_product(bank(2 + m % 2), W3T, m * P, P, FH, b).then_inc(s["up"], 1)
                        if preparing:
                            self.prepare_rest(m, 1)
                    if m in (FM - 1, FM):
                        if preparing:
                            pe.wait_ge(rest_ev, len(PREP_REST))
                            pe.wait_ge(rest_low, REST_LOWS[-1])
                        self.norm_transpose(it + 2, m - (FM - 1), at=(7, 4)[m - (FM - 1)])
                    if m == 2:
                        self.open_output(it)
                    if m >= 2:
                        if preparing:
                            pe.wait_ge(had_ev, FM // 2)
                        self.down_chunk(s, b, FM, m - 2, P, W2T, (m - 2) * D)
                    if preparing and m == 1:
                        self.prepare_w2()
                    if preparing:
                        self.prepare_rest(m, 2)

            def moe(self, st, b):
                pe, s, it = self.pe, S[st], 2 * st + b
                split = 0 if st == MOE0 else MM + 1
                pe.wait_ge(xnT_ev, 2 * it + 2)
                self.input_product(bank(7)[0:NE, :], (gateT[:, 0:DC * NE], gateT[:, DC * NE:]), 0, NE, NE, b)\
                    .then_inc(s["score"], 1)

                def broadcast_weight(p, m):
                    pe.wait_ge(s["combT"], b + 1)
                    pe.wait_ge(s["prod"], HEAD + b * MM + p)
                    nc.tensor.matmul(bank(4), expert_b[0:3 * NE, m * P:(m + 1) * P], combT[0:3 * NE, :],
                                     start=True, stop=True).then_inc(s["cb"], 1)

                for p in range(MM + 2):
                    if p < MM:
                        m = MOE_ORDER[p]
                        rows = LAST_ROWS if m == MM - 1 else P
                        if p != 1:
                            pe.wait_ge(s["prod"], HEAD + b * MM + max(p - 1, 0))
                        pe.wait_ge(moe_split, split + p + 1)
                        self.input_product(bank(p % 2)[0:rows, :], w1h, m * P, rows, MH, b)
                        self.input_product(bank(2 + p % 2)[0:rows, :], w3h, m * P, rows, MH, b)\
                            .then_inc(s["up"], 1)
                    if p in (MM - 2, MM - 1) and (st == MOE0 or b == 0):
                        self.norm_transpose(it + 2, p - (MM - 2))
                    if p == MM:
                        pe.wait_ge(moe_split, split + MM + 1)
                    if p == 0:
                        pe.wait_ge(s["sig"], b + 1)
                        for tc in range(TC):
                            last = nc.tensor.matmul(bank(7)[:, tc * NE:(tc + 1) * NE],
                                                    sigT[0:NE, tc * P:(tc + 1) * P], ident[0:NE, 0:NE],
                                                    start=True, stop=True)
                        last.then_inc(s["sigt"], 1)
                    if p == 2:
                        self.open_output(it)
                        pe.wait_ge(s["comb"], b + 1)
                        parts = route[:, COMB_AT:COMB_AT + TC * 3 * NE // 2].bitcast(BF16)
                        for tc in range(TC):
                            last = nc.tensor.transpose(bank(7)[0:3 * NE, :].bitcast(BF16)[:, tc * P:(tc + 1) * P],
                                                       parts[:, tc * 3 * NE:(tc + 1) * 3 * NE], ident_b[:, :])
                        last.then_inc(s["combt"], 1)
                    if 2 < p < MM:
                        broadcast_weight(p, m)
                    if p >= 2:
                        d = MOE_ORDER[p - 2]
                        self.down_chunk(s, b, MM, p - 2, LAST_ROWS if d == MM - 1 else P, (w2_hi, w2_lo), d * D)
                    if p == 2:
                        broadcast_weight(p, m)

            def mamba(self, b):
                pe, s, it = self.pe, S[MAMBA], 2 * MAMBA + b

                def project(o, w, width, k):
                    return nc.tensor.matmul(o[0:width, :], w[:, k * width:(k + 1) * width],
                                            xc[:, k * T:(k + 1) * T], start=(k == 0), stop=(k == EC - 1))

                pe.wait_ge(rest_ev, len(PREP_REST))
                pe.wait_ge(rest_low, REST_LOWS[-1])
                pe.wait_ge(xnT_ev, 2 * it + 2)
                for c in range(2 * EC):
                    if c == EC + 1:
                        pe.wait_ge(resid_done, HEAD + it)
                    if c == 2 * EC - 1:
                        for k in range(EC):
                            pe.wait_ge(s["xc"], b * EC + k + 1)
                            last = project(bank(0), WxdT, DTR, k)
                        last.then_inc(s["dt"], 1)
                    self.input_product(bank(c), WinT, c * P, P, 2 * DI, b).then_inc(s["xp"] if c < EC else s["z"], 1)
                pe.wait_ge(s["dtT"], b + 1)
                for c in SOFTPLUS_ORDER:
                    if 2 + c >= EC:
                        pe.wait_ge(s["zs"], b * EC + 2 + c - EC + 1)
                    nc.tensor.matmul(bank(2 + c), WdtT[:, c * P:(c + 1) * P], dtT, start=True, stop=True)\
                        .then_inc(s["dl"], 1)
                for k in range(EC):
                    last = project(bank(1), WxbT, 96, k)
                last.then_inc(s["bc"], 1)

                def broadcast_b(half, n, u):
                    pe.wait_ge(s["mul"], HEAD + (b * 2 + half) * DS + n - 1)
                    nc.tensor.matmul(bank(u % 2), pick[0:96, bass.ds(n, 1)].broadcast_to([96, P]),
                                     bc_stack[0:96, :], start=True, stop=True).then_inc(s["B"], 1)

                def broadcast_c(half, n, u):
                    pe.wait_ge(s["cev"], HEAD + (b * 2 + half) * DS + n - 1)
                    nc.tensor.matmul(bank(2 + u % 2), pick[0:96, bass.ds(n + DS, 1)].broadcast_to([96, P]),
                                     bc_stack[0:96, :], start=True, stop=True).then_inc(s["C"], 1)

                def add_state(half, n, slot, stop=False):
                    pe.wait_ge(s["hc"], HEAD + (b * 2 + half) * DS + n + 1)
                    for j in range(2):
                        last = nc.tensor.matmul(bank(SUM_BANKS[half][j]), ident[:, :],
                                                hc[:, slot * 2 * T + j * T:slot * 2 * T + (j + 1) * T],
                                                start=False, stop=stop)
                    last.then_inc(s["ys"], 1)

                pe.wait_ge(s["stack"], b + 1)
                broadcast_b(0, 0, 0)
                pe.wait_ge(s["abs"], (b + 1) * EC)
                pe.wait_ge(s["dx"], (b + 1) * 2)
                for half in range(2):
                    for j in range(2):
                        nc.tensor.matmul(bank(SUM_BANKS[half][j]), ident_b[:, :], zero_b[:, :],
                                         start=True, stop=False)

                    def quad(q, first=False, final=False):
                        for u in range(4):
                            n = q * 4 + u
                            if u < 3 or not final:
                                broadcast_b(half, n + 1, u + 1)
                            elif half == 0:
                                broadcast_b(1, 0, 0)
                            broadcast_c(half, n, u)
                            if not first:
                                add_state(half, n - 4, u)
                            elif half:
                                add_state(0, DS - 4 + u, u, stop=(u == 3))

                    quad(0, first=True)
                    with pe.Fori(1, DS // 4 - 1) as q:
                        quad(q)
                    quad(DS // 4 - 1, final=True)

                def output(c):
                    for tc in range(TC):
                        last = nc.tensor.matmul(bank(5 + tc // 2)[:, (tc % 2) * D:(tc % 2 + 1) * D],
                                                zs[:, c * T + tc * P:c * T + (tc + 1) * P],
                                                WoutT[:, c * D:(c + 1) * D], start=False,
                                                stop=(c == EC - 1 and tc % 2 == 1))
                    return last

                pe.wait_ge(s["yf"], b * 3 + 1)
                for j in range(2):
                    nc.tensor.matmul(bank(5 + j), ident_b[:, :], zero_b[:, :], start=True, stop=False)
                for u in range(4):
                    if u == 0:
                        output(0)
                    add_state(1, DS - 4 + u, u, stop=(u == 3))
                output(1)
                pe.wait_ge(s["mul"], HEAD + (b + 1) * 2 * DS)
                for ch in range(DC):
                    self.norm_transpose(it + 2, ch, at=ch)
                for c in (2, 3):
                    pe.wait_ge(s["yf"], b * 3 + c)
                    last = output(c)
                last.then_inc(down_done, 1)

            def attention(self, b):
                pe, s, it = self.pe, S[ATTN], 2 * ATTN + b
                pe.wait_ge(xnT_ev, 2 * it + 2)
                for n, (w, c) in enumerate(((WqT, 0), (WkT, 0), (WqT, 1), (WkT, 1), (WvT, 0), (WvT, 1))):
                    if n == 5:
                        pe.wait_ge(resid_done, HEAD + it)
                    self.input_product(bank(n), w, c * P, P, D, b).then_inc(s["qkv"], 1)
                for c in range(DC):
                    pe.wait_ge(s["v_ev"], b * DC + c + 1)
                    for tc in range(TC):
                        last = nc.tensor.transpose(bank(6 - 2 * c)[:, tc * P:(tc + 1) * P],
                                                   v32[:, c * T + tc * P:c * T + (tc + 1) * P], ident[:, :])
                    last.then_inc(s["vt"], 1)

                def scores_by_query(first, end, quad, before):
                    with pe.Fori(first, end) as g:
                        for qc in range(TC):
                            n = (qc + 1) * P
                            pe.wait_ge(s["max"], HEAD + b * 32 + g * 4 + qc - 3)
                            if qc == 0:
                                pe.wait_ge(s[f"stacked{quad}"], (b + 1) * 16 * 6)
                                for sm, count in before:
                                    pe.wait_ge(sm, count)
                            for j in range(2):
                                o = bank(2 * qc + j)
                                nc.tensor.matmul(o[:, 0:n], q_stack[0:MAX_ROW, bass.ds((g * 2 + j) * T + qc * P, P)],
                                                 k_stack[0:MAX_ROW, bass.ds((g * 2 + j) * T, n)],
                                                 start=True, stop=False)
                                last = nc.tensor.matmul(o[:, n - P:n], ident_b[:, :], mask_q[:, :],
                                                        start=False, stop=True)
                            last.then_inc(s["s1"], 1)

                def maxima_to_rows(half):
                    pe.wait_ge(s["mparts"], b * HALVES + half + 1)
                    w = 3 * HH * TC
                    nc.tensor.transpose(bank(MAX_BANKS[half]).bitcast(BF16)[0:w, 0:P],
                                        m_parts[:, half * w:(half + 1) * w], ident_b[:, :]).then_inc(s["mt"], 1)

                pairs = NH // 2
                scores_by_query(0, 2, 0, ((ld["aux"], 16 * 2), (s["rest"], rest_at(b, 1, "q32")),
                                          (s["cast"], cast_at(b, 1, "k32")), (s["vtok"], (b + 1) * DC)))
                scores_by_query(2, 4, 1, ())
                scores_by_query(4, 5, 2, ())
                pe.wait_ge(s["max"], HEAD + (b * 32 + (pairs // 2) * 4 + 1))
                maxima_to_rows(0)
                scores_by_query(5, 6, 2, ((s["mrows"], b * HALVES + 1),))
                scores_by_query(6, pairs, 3, ())

                def scores(hq, j, first=False):
                    pe.wait_ge(s["p"], HEAD + b * NH + hq * 4 + (j - 1))
                    if j == 0:
                        if first:
                            pe.wait_ge(s["max"], HEAD + ((b + 1) * 32 - 2))
                        for half in range(1 if first else HALVES):
                            pe.wait_ge(s[f"mstacked{half}"], (b + 1) * 16)
                    for kc in range(TC):
                        n = TILE_COLS[kc]
                        o = bank(3 * (j % 2), 3)[:, TILE_AT[kc]:TILE_AT[kc] + n]
                        keys = k_stack[0:STACK, bass.ds((hq * 4 + j) * T + kc * P, P)]
                        nc.tensor.matmul(o, keys, q_stack[0:STACK, bass.ds((hq * 4 + j) * T + kc * P, n)],
                                         start=True, stop=False)
                        last = nc.tensor.matmul(o[:, 0:P], ident_b[:, :], mask_k[:, :], start=False, stop=True)
                    last.then_inc(s["s2"], 1)

                def values(hq, j):
                    pe.wait_ge(s["p"], HEAD + b * NH + hq * 4 + (j + 1))
                    if j == 0:
                        pe.wait_ge(s["v4"], b * 4 + hq + 1)
                        pe.wait_ge(s["o4"], HEAD + b * 4 + hq)
                    for kc in range(TC):
                        n = TILE_COLS[kc]
                        at = (j % 2) * PT_COLS + TILE_AT[kc]
                        last = nc.tensor.matmul(bank(6)[32 * j:32 * j + 32, kc * P:T],
                                                v_four[:, (kc * 4 + j) * 32:(kc * 4 + j + 1) * 32],
                                                pT[:, at:at + n], start=(kc == 0), stop=(kc == TC - 1))
                    last.then_inc(s["av"], 1)

                def outputs_to_tokens(hq):
                    pe.wait_ge(s["o4"], HEAD + b * 4 + hq + 1)
                    pe.wait_ge(s["otok"], HEAD + b * 4 + hq)
                    pe.wait_ge(s["mrows"], (b + 1) * HALVES)
                    for tc in range(TC):
                        last = nc.tensor.transpose(bank(7)[:, tc * P:(tc + 1) * P], o_four[:, tc * P:(tc + 1) * P],
                                                   ident[:, :])
                    last.then_inc(s["ot"], 1)

                def group(hq, first=False, final=False):
                    scores(hq, 1)
                    values(hq, 0)
                    scores(hq, 2)
                    if not first:
                        outputs_to_tokens(hq - 1)
                    values(hq, 1)
                    scores(hq, 3)
                    values(hq, 2)
                    if not final:
                        scores(hq + 1, 0)
                    values(hq, 3)

                groups = NH // 4
                scores(0, 0, first=True)
                maxima_to_rows(1)
                group(0, first=True)
                with pe.Fori(1, groups - 1) as hq:
                    group(hq)
                group(groups - 1, final=True)
                pe.wait_ge(s["p"], HEAD + (b + 1) * NH)
                for ch in range(DC):
                    self.norm_transpose(it + 2, ch, at=2 + ch)
                outputs_to_tokens(groups - 1)
                pe.wait_ge(s["otok"], HEAD + b * 4 + 4)
                for c in range(DC):
                    for tc in range(TC):
                        last = nc.tensor.transpose(bank(c)[:, tc * P:(tc + 1) * P],
                                                   o_tok[:, tc * D + c * P:tc * D + (c + 1) * P], ident[:, :])
                    last.then_inc(s["oT_up"], 1)
                pe.wait_ge(s["oT"], b * DC + DC)
                self.down(it, [(P, oT[:, c * T:(c + 1) * T], WoT[:, c * D:(c + 1) * D]) for c in range(DC)],
                          bias=True)

        class ScalarProgram:
            def __init__(self, act):
                self.act = act

            def prepare(self):
                act = self.act
                nc.scalar.preload_act_table(ACT.Sqrt)
                self.norm_sd(1)
                for n, (_, _, dst) in enumerate(PREP_FIRST):
                    act.wait_ge(prep_tr, n + 1)
                    o, src = evacuation(bank(n % 4), dst)
                    nc.scalar.activation(o, src, ACT.Copy).then_inc(prep_ev, 1)
                self.norm_evacuate(1, 0)

            def prepare_w2(self):
                act = self.act
                for g in range(FM // 2):
                    act.wait_ge(w2_up, g + 1)
                    nc.scalar.activation(w2_raw2[:, g * 512:(g + 1) * 512], side_bank(g), ACT.Copy)\
                        .then_inc(w2_ev, 1)
                for g in range(FM // 2):
                    act.wait_ge(had_up, g + 1)
                    nc.scalar.activation(W2T[0][:, g * 512:(g + 1) * 512], side_bank(g), ACT.Copy).then_inc(had_hi, 1)

            def prepare_rest(self, m, i):
                for n in rest_groups(m, i):
                    self.act.wait_ge(rest_tr, n + 1)
                    o, src = evacuation(side_bank(n), PREP_REST[n][2])
                    nc.scalar.activation(o, src, ACT.Copy).then_inc(rest_ev, 1)

            def prepare_decay(self):
                act = self.act
                act.wait_ge(ld["cols"], 16 * COL_LOADS)
                nc.scalar.activation(c_A, c_A, ACT.Exp).then_inc(a_ready, 1)
                act.wait_ge(a_ready, 1)
                nc.scalar.mul(c_A, c_A, -1.0).then_inc(a_ready, 1)

            def norm_evacuate(self, k, target, chunks=range(DC), banks=(7, 7)):
                for ch in chunks:
                    self.act.wait_ge(xnT_tr, 2 * (k - 1) + ch + 1)
                    nc.scalar.activation(xnT_hi[:, bass.ds(target * DC * T + ch * T, T)], bank(banks[ch]), ACT.Copy)\
                        .then_inc(xnT_high, 1)

            def norm_sd(self, k):
                nc.scalar.preload_act_table(ACT.Sqrt)
                self.act.wait_ge(var_ready, k)
                nc.scalar.activation(stats[:, 36:40], stats[:, 32:36], ACT.Sqrt).then_inc(sd_ready, 1)

            def gate(self, s, b, count, p, rows=P):
                act, slot = self.act, p % 2
                act.wait_ge(s["up"], b * count + p + 1)
                act.wait_ge(s["hid"], HEAD + b * count + max(p - 1, 0))
                nc.scalar.activation(gated[0:rows, slot * T:(slot + 1) * T], bank(slot)[0:rows, :], ACT.Silu)\
                    .then_inc(s["silu"], 1)

            def high(self, s, b, count, p, rows=P):
                act, slot = self.act, p % 2
                act.wait_ge(s["prod"], HEAD + b * count + p + 1)
                act.wait_ge(s["used"], HEAD + b * (count - 1) + max(p - RING + 1, 0))
                nc.scalar.activation(ring[p % RING][0][0:rows, :], gated[0:rows, slot * T:(slot + 1) * T], ACT.Copy)\
                    .then_inc(s["high"], 1)

            def ffn(self, st, b):
                act, s, it = self.act, S[st], 2 * st + b
                preparing = st == FFN0 and b == 0
                nc.scalar.preload_act_table(ACT.Silu)
                self.gate(s, b, FM, 0)
                for p in range(1, FM + 1):
                    if p == FM // 2:
                        self.norm_sd(it + 2)
                        nc.scalar.preload_act_table(ACT.Silu)
                    if preparing:
                        self.prepare_rest(p, 0)
                    if p < FM:
                        self.gate(s, b, FM, p)
                    if preparing:
                        self.prepare_rest(p, 1)
                    self.high(s, b, FM, p - 1)
                    if p >= FM - 1:
                        self.norm_evacuate(it + 2, 1 - b, (p - (FM - 1),), banks=(7, 4))
                    if preparing and p == 1:
                        self.prepare_w2()
                    if preparing:
                        self.prepare_rest(p, 2)
                if preparing:
                    self.prepare_decay()

            def moe(self, st, b):
                act, s, it = self.act, S[st], 2 * st + b

                def rows(p):
                    return LAST_ROWS if MOE_ORDER[p] == MM - 1 else P

                nc.scalar.preload_act_table(ACT.Exp)
                act.wait_ge(s["score"], b + 1)
                nc.scalar.activation(sigT[0:NE, :], bank(7)[0:NE, :], ACT.Exp, scale=-1.0).then_inc(s["sig"], 1)
                nc.scalar.preload_act_table(ACT.Silu)
                self.gate(s, b, MM, 0, rows(0))
                self.gate(s, b, MM, 1, rows(1))
                self.high(s, b, MM, 0, rows(0))
                for p in range(2, MM + 1):
                    if p == 3:
                        act.wait_ge(s["combt"], b + 1)
                        nc.scalar.activation(combT[0:3 * NE, :], bank(7)[0:3 * NE, :].bitcast(BF16)[:, 0:T],
                                             ACT.Copy).then_inc(s["combT"], 1)
                    if p == MM // 2 and (st == MOE0 or b == 0):
                        self.norm_sd(it + 2)
                        nc.scalar.preload_act_table(ACT.Silu)
                    if p < MM:
                        self.gate(s, b, MM, p)
                    self.high(s, b, MM, p - 1, rows(p - 1))
                    if p in (MM - 2, MM - 1) and (st == MOE0 or b == 0):
                        self.norm_evacuate(it + 2, 1 - b, (p - (MM - 2),))

            def mamba(self, b):
                act, s, it = self.act, S[MAMBA], 2 * MAMBA + b
                act.wait_ge(rest_ev, len(PREP_REST))
                act.wait_ge(col_ready, 1)
                nc.scalar.preload_act_table(ACT.Silu)

                def chunk(t, c):
                    return t[:, c * T:(c + 1) * T]

                for c in range(EC + 2):
                    if c < EC:
                        act.wait_ge(s["xp"], b * EC + c + 1)
                        nc.scalar.activation(chunk(xc, c), bank(c), ACT.Identity, bias=c_convb[:, c:c + 1],
                                             scale=c_convw[:, c * DCONV + 3:c * DCONV + 4]).then_inc(s["ini"], 1)
                    if c >= 2:
                        act.wait_ge(s["tap"], tap_at(b, c - 2, 0))
                        nc.scalar.activation(chunk(xc, c - 2), chunk(xc, c - 2), ACT.Silu).then_inc(s["xc"], 1)
                for c in range(EC):
                    if c == EC - 1:
                        act.wait_ge(s["dt"], b + 1)
                        nc.scalar.activation(dtT, bank(0), ACT.Copy).then_inc(s["dtT"], 1)
                    act.wait_ge(s["z"], b * EC + c + 1)
                    nc.scalar.activation(chunk(zs, c), bank(EC + c), ACT.Silu).then_inc(s["zs"], 1)
                nc.scalar.preload_act_table_set("natural_log_exp_and_others")

                def softplus_parts(c):
                    act.wait_ge(s["dl"], b * EC + SOFTPLUS_RANK[c] + 1)
                    if c not in SOFTPLUS_DVE:
                        nc.scalar.activation(sp_pos[c], bank(2 + c), ACT.Relu, bias=c_bdt[:, c:c + 1])
                    nc.scalar.activation(chunk(delta, c), bank(2 + c), ACT.Abs, bias=c_bdt[:, c:c + 1])\
                        .then_inc(s["abs"], 1)
                    act.wait_ge(s["abs"], b * EC + SOFTPLUS_RANK[c] + 1)
                    nc.scalar.activation(chunk(delta, c), chunk(delta, c), ACT.Exp, scale=-1.0).then_inc(s["e"], 1)
                    act.wait_ge(s["e"], b * EC + SOFTPLUS_RANK[c] + 1)
                    nc.scalar.activation(chunk(dx, c), chunk(delta, c), ACT.Ln, bias=1.0).then_inc(s["ln"], 1)
                    if c not in SOFTPLUS_DVE:
                        low = sp_low[c]
                        nc.scalar.activation(low, chunk(delta, c), ACT.Identity, bias=1.0).then_inc(s["u"], 1)
                        act.wait_ge(s["u"], b * 4 + (2 * SOFTPLUS_POOL.index(c) + 1))
                        nc.scalar.activation(low, low, ACT.Identity, bias=minus_one).then_inc(s["u"], 1)

                for c in SOFTPLUS_ORDER:
                    softplus_parts(c)
                act.wait_ge(s["col0"], b + 1)
                act.wait_ge(a_ready, 2)

                def step(half, n, u):
                    at = (b * 2 + half) * DS + n
                    act.wait_ge(s["scan"], HEAD + at - 1)
                    for j in range(2):
                        c = 2 * half + j
                        last = nc.scalar.activation(decay[u % 2][:, j * T + 1:(j + 1) * T],
                                                    delta[:, c * T + 1:(c + 1) * T], ACT.Exp,
                                                    scale=c_A[:, bass.ds(n + c * DS, 1)])
                    last.then_inc(s["dA"], 1)
                    act.wait_ge(s["C"], at + 1)
                    act.wait_ge(s["hc"], HEAD + at - 1)
                    nc.scalar.activation(c_bc[:, (u % 2) * T:(u % 2 + 1) * T], bank(2 + u % 2), ACT.Copy)\
                        .then_inc(s["cev"], 1)

                for half in range(2):
                    act.wait_ge(s[("dx", "dx_p")[half]], (b + 1) * 2)
                    for u in range(4):
                        step(half, u, u)
                    with act.Fori(1, DS // 4) as q:
                        for u in range(4):
                            step(half, q * 4 + u, u)
                self.norm_sd(it + 2)
                self.norm_evacuate(it + 2, 1 - b, banks=(0, 1))

            def attention(self, b):
                act, s, it = self.act, S[ATTN], 2 * ATTN + b

                def chunk(t, c):
                    return t[:, c * T:(c + 1) * T]

                def cast(c, name, dst, src, needs):
                    act.wait_ge(s["rest"], rest_at(b, c, needs))
                    nc.scalar.activation(dst, src, ACT.Copy).then_inc(s["cast"], 1)

                def keys(c):
                    act.wait_ge(s["qkv"], b * 6 + 2 * c + 2)
                    nc.scalar.activation(chunk(k32, c), bank(2 * c + 1), ACT.Identity, bias=c_bk[:, c:c + 1])\
                        .then_inc(s["cast"], 1)

                def split(c):
                    k, q = chunk(k32, c), chunk(q32, c)
                    act.wait_ge(s["cast"], cast_at(b, c, "k32"))
                    nc.scalar.activation(part_of(k_parts, c, 0), k, ACT.Copy).then_inc(s["cast"], 1)
                    cast(c, "q_hi", part_of(q_parts, c, 0), q, "q32")
                    cast(c, "k_mid", part_of(k_parts, c, 1), k, "k_1")
                    cast(c, "q_mid", part_of(q_parts, c, 1), q, "q_1")
                    cast(c, "k_lo", part_of(k_parts, c, 2), k, "k_2")
                    cast(c, "q_lo", part_of(q_parts, c, 2), q, "q_2")

                keys(0)
                split(0)
                keys(1)
                self.norm_sd(it + 2)
                for c in range(DC):
                    act.wait_ge(s["qkv"], b * 6 + 5 + c)
                    nc.scalar.activation(chunk(v32, c), bank(4 + c), ACT.Identity, bias=c_bv[:, c:c + 1])\
                        .then_inc(s["v_ev"], 1)
                for c in range(DC):
                    act.wait_ge(s["vt"], b * DC + c + 1)
                    nc.scalar.activation(v_tok.rearrange("p (t d) -> p t d", t=TC)[:, :, c * P:(c + 1) * P],
                                         bank(6 - 2 * c).rearrange("p (t d) -> p t d", t=TC), ACT.Copy)\
                        .then_inc(s["vtok"], 1)
                split(1)
                nc.scalar.preload_act_table(ACT.Exp)
                for half in range(HALVES):
                    act.wait_ge(s["mt"], b * HALVES + half + 1)
                    nc.scalar.activation(m_rows[0:3 * HH * TC, half * P:(half + 1) * P],
                                         bank(MAX_BANKS[half]).bitcast(BF16)[0:3 * HH * TC, 0:P], ACT.Copy)\
                        .then_inc(s["mrows"], 1)

                def exponential(hq, j):
                    act.wait_ge(s["s2"], b * NH + hq * 4 + (j + 1))
                    act.wait_ge(s["av"], HEAD + b * NH + hq * 4 + (j - 1))
                    nc.scalar.activation(pT[:, (j % 2) * PT_COLS:(j % 2 + 1) * PT_COLS],
                                         bank(3 * (j % 2), 3)[:, 0:PT_COLS], ACT.Exp).then_inc(s["p"], 1)

                def group(hq, final=False):
                    for j in range(1, 4):
                        exponential(hq, j)
                    if not final:
                        exponential(hq + 1, 0)
                    act.wait_ge(s["av"], HEAD + b * NH + hq * 4 + 4)
                    act.wait_ge(s["ot"], HEAD + b * 4 + hq)
                    nc.scalar.activation(o_four, bank(6), ACT.Copy).then_inc(s["o4"], 1)

                exponential(0, 0)
                with act.Fori(0, NH // 4 - 1) as hq:
                    group(hq)
                group(NH // 4 - 1, final=True)
                self.norm_evacuate(it + 2, 1 - b, banks=(2, 3))
                for c in range(DC):
                    act.wait_ge(s["oT_up"], b * DC + c + 1)
                    nc.scalar.activation(oT[:, c * T:(c + 1) * T], bank(c), ACT.Copy).then_inc(s["oT"], 1)

        class VectorProgram:
            def __init__(self, dve):
                self.dve = dve
                self.base = 0
                self.n = 0
                self.passes = 0

            def link(self, ins):
                self.n += 1
                ins.then_inc(dve_chain, 1)
                self.dve.wait_ge(dve_chain, self.passes + (self.base + self.n))

            def stage(self, body, links, peeled=False):
                def one(b):
                    self.n, self.passes = 0, b * links
                    body(b)
                    assert self.n == links or (peeled and b and self.n < links), (self.n, links)
                over_batches(self.dve, one, peeled)
                self.base += NB * links
                self.n, self.passes = 0, 0

            def prepare(self):
                dve = self.dve
                nc.vector.memset(minus_one, -1.0)
                nc.vector.memset(cols[:, 49:50], 0.0)
                nc.vector.memset(ones_row[0:1, :], 1.0).then_inc(col_ready, 1)
                dve.wait_ge(ld["x0"], 16)
                self.norm(0, 1)
                for n, (_, _, dst) in enumerate(PREP_FIRST):
                    dve.wait_ge(prep_ev, n + 1)
                    nc.vector.tensor_tensor(dst[3], evacuation(bank(n % 4), dst)[1], dst[1], ALU.subtract)\
                        .then_inc(prep_low, 1)
                self.norm_low(1, 0)
                dve.wait_ge(ld["W2"], 16)
                src, dst = w2_raw, w2_mix
                for i, h in enumerate((1, 2, 4)):
                    def pair(t, side):
                        return t.rearrange("p (g s r) -> p g s r", s=2, r=h * P)[:, :, side, :]
                    for side, op in ((0, ALU.add), (1, ALU.subtract)):
                        last = nc.vector.tensor_tensor(pair(dst, side), pair(src, 0), pair(src, 1), op)
                        last.then_inc(w2_mixed, 1)
                    dve.wait_ge(w2_mixed, 2 * i + 2)
                    src, dst = dst, src

            def prepare_w2(self):
                for g in range(FM // 2):
                    self.dve.wait_ge(had_hi, g + 1)
                    w = slice(g * 512, (g + 1) * 512)
                    nc.vector.tensor_tensor(W2T[1][:, w], side_bank(g), W2T[0][:, w], ALU.subtract)\
                        .then_inc(had_ev, 1)

            def prepare_rest(self, m, i):
                for n in rest_groups(m, i):
                    dst = PREP_REST[n][2]
                    if dst[3] is not None:
                        self.dve.wait_ge(rest_ev, n + 1)
                        nc.vector.tensor_tensor(dst[3], evacuation(side_bank(n), dst)[1], dst[1], ALU.subtract)\
                            .then_inc(rest_low, 1)

            def norm(self, b, k, free=None):
                dve = self.dve
                rows = [x_tok[:, bass.ds((b * TC + tc) * D, D)] for tc in range(TC)]
                nc.vector.memset(stats[:, 44:45], 0.0)
                for tc in range(TC):
                    last = nc.vector.bn_stats(stats[:, tc * 6:(tc + 1) * 6], rows[tc])
                self.link(last)
                nc.vector.memset(stats[:, 44:45], 0.0)
                for tc in range(TC):
                    last = nc.vector.bn_aggr(stats[:, 24 + 2 * tc:26 + 2 * tc], stats[:, tc * 6:(tc + 1) * 6])
                self.link(last)
                var = stats[:, 24:32].rearrange("p (t s) -> p t s", s=2)[:, :, 1]
                nc.vector.tensor_scalar_add(stats[:, 32:36], var, EPS).then_inc(var_ready, 1)
                dve.wait_ge(sd_ready, k)
                self.link(nc.vector.reciprocal(stats[:, 40:44], stats[:, 36:40]))
                dve.wait_ge(xnT_tr, 2 * (k - 1))
                if free:
                    dve.wait_ge(*free)
                for tc in range(TC):
                    last = nc.vector.tensor_scalar(xn_tok[:, tc * D:(tc + 1) * D], rows[tc],
                                                   stats[:, 24 + 2 * tc:25 + 2 * tc], stats[:, 40 + tc:41 + tc],
                                                   ALU.subtract, ALU.mult)
                last.then_inc(xn_done, 1)

            def norm_low(self, k, target, chunks=range(DC), banks=(7, 7)):
                for ch in chunks:
                    self.dve.wait_ge(xnT_high, 2 * (k - 1) + ch + 1)
                    x_ = bass.ds(target * DC * T + ch * T, T)
                    nc.vector.tensor_tensor(xnT_lo[:, x_], bank(banks[ch]), xnT_hi[:, x_], ALU.subtract)\
                        .then_inc(xnT_ev, 1)

            def residual(self, it, b, scale):
                dve = self.dve
                dve.wait_ge(down_done, it + 1)
                for h in range(2):
                    r = x_tok[:, bass.ds((b * TC + 2 * h) * D, 2 * D)]
                    last = nc.vector.scalar_tensor_tensor(r, bank(5 + h), scale, r, ALU.mult, ALU.add)
                last.then_inc(resid_done, 1)
                dve.wait_ge(resid_done, HEAD + it + 1)

            def times_gate(self, s, b, count, p, rows=P):
                slot = p % 2
                g = gated[0:rows, slot * T:(slot + 1) * T]
                self.dve.wait_ge(s["silu"], b * count + p + 1)
                return nc.vector.tensor_tensor(g, g, bank(2 + slot)[0:rows, :], ALU.mult)

            def low(self, s, b, count, p, rows=P):
                slot = p % 2
                self.dve.wait_ge(s["high"], b * count + p + 1)
                hi, lo = ring[p % RING]
                nc.vector.tensor_tensor(lo[0:rows, :], gated[0:rows, slot * T:(slot + 1) * T], hi[0:rows, :],
                                        ALU.subtract).then_inc(s["hid"], 1)

            def ffn(self, st, b):
                s, it = S[st], 2 * st + b
                preparing = st == FFN0 and b == 0
                for p in range(FM + 1):
                    if p == FM // 2:
                        if preparing:
                            self.dve.wait_ge(ld["x1"], 16)
                        self.norm(1 - b, it + 2)
                    if preparing:
                        self.prepare_rest(p, 0)
                    if p < FM:
                        self.times_gate(s, b, FM, p).then_inc(s["prod"], 1)
                    if preparing:
                        self.prepare_rest(p, 1)
                    if p:
                        self.low(s, b, FM, p - 1)
                    if p >= FM - 1:
                        self.norm_low(it + 2, 1 - b, (p - (FM - 1),), banks=(7, 4))
                    if preparing and p == 1:
                        self.prepare_w2()
                    if preparing:
                        self.prepare_rest(p, 2)
                self.residual(it, b, 0.5)

            def moe(self, st, b):
                dve, s, it = self.dve, S[st], 2 * st + b

                def rows(p):
                    return LAST_ROWS if MOE_ORDER[p] == MM - 1 else P

                self.times_gate(s, b, MM, 0, rows(0)).then_inc(s["prod"], 1)
                self.route_weights(s, b)
                self.low(s, b, MM, 0, rows(0))
                self.times_gate(s, b, MM, 1, rows(1)).then_inc(s["prod"], 1)
                for p in range(2, MM + 1):
                    if p == MM // 2 and (st == MOE0 or b == 0):
                        self.norm(1 - b, it + 2)
                    if p < MM:
                        self.times_gate(s, b, MM, p).then_inc(s["mixed"], 1)
                        dve.wait_ge(s["mixed"], b * RC + p - 1)
                        dve.wait_ge(s["cb"], b * RC + p - 1)
                        g = gated[:, (p % 2) * T:(p % 2 + 1) * T]
                        nc.vector.tensor_tensor(g, g, bank(4), ALU.mult).then_inc(s["prod"], 1)
                    self.low(s, b, MM, p - 1, rows(p - 1))
                    if p in (MM - 2, MM - 1) and (st == MOE0 or b == 0):
                        self.norm_low(it + 2, 1 - b, (p - (MM - 2),))
                self.residual(it, b, 0.5)

            def route_weights(self, s, b):
                dve, v = self.dve, nc.vector
                n = TC * NE
                score, weight = route[:, 0:n], route[:, n:2 * n]
                rank, rest = route[:, 2 * n:3 * n], route[:, 3 * n:4 * n]
                total = route[:, 4 * n:4 * n + TC]
                above = route[:, 256:256 + n * NE]
                equal = route[:, 512:512 + n * NE]

                def grid(t):
                    return t.rearrange("p (t e f) -> p t e f", t=TC, e=NE)

                s3 = score.rearrange("p (t e) -> p t e", t=TC)
                other = s3.unsqueeze(2).broadcast_to([P, TC, NE, NE])
                own = s3.unsqueeze(3).broadcast_to([P, TC, NE, NE])
                dve.wait_ge(s["sigt"], b + 1)
                self.link(v.tensor_scalar_add(score, bank(7)[:, 0:n], 1.0))
                self.link(v.reciprocal(score, score))
                self.link(v.tensor_tensor(grid(above), other, own, ALU.is_gt))
                self.link(v.tensor_tensor(grid(equal), other, own, ALU.is_equal))
                eq = equal.rearrange("p (t f) -> p t f", t=TC)
                self.link(v.tensor_tensor(eq, eq, lower.unsqueeze(1).broadcast_to([P, TC, NE * NE]), ALU.mult))
                self.link(v.tensor_tensor(above, above, equal, ALU.add))
                self.link(v.reduce_sum(rank, above.rearrange("p (a f) -> p a f", f=NE), AX.X))
                self.link(v.scalar_tensor_tensor(weight, rank, 1.5, score, ALU.is_lt, ALU.mult))
                w3d = weight.rearrange("p (t e) -> p t e", t=TC)
                self.link(v.reduce_sum(total, w3d, AX.X))
                self.link(v.tensor_scalar_add(total, total, 1e-20))
                self.link(v.reciprocal(total, total))
                self.link(v.tensor_scalar(total, total, 2.5, None, ALU.mult))
                self.link(v.tensor_tensor(w3d, w3d, total.unsqueeze(2).broadcast_to([P, TC, NE]), ALU.mult))
                parts = route[:, COMB_AT:COMB_AT + n * 3 // 2].bitcast(BF16)\
                    .rearrange("p (t i e) -> p t i e", t=TC, i=3)
                r3 = rest.rearrange("p (t e) -> p t e", t=TC)
                self.link(v.tensor_copy(parts[:, :, 0, :], w3d))
                self.link(v.tensor_tensor(r3, w3d, parts[:, :, 0, :], ALU.subtract))
                self.link(v.tensor_copy(parts[:, :, 1, :], r3))
                self.link(v.tensor_tensor(r3, r3, parts[:, :, 1, :], ALU.subtract))
                v.tensor_copy(parts[:, :, 2, :], r3).then_inc(s["comb"], 1)

            def mamba(self, b):
                dve, v, s, it = self.dve, nc.vector, S[MAMBA], 2 * MAMBA + b
                dve.wait_ge(rest_ev, len(PREP_REST))
                for t in decay:
                    last = v.memset(t.rearrange("p (c t) -> p c t", t=T)[:, :, 0:1], 0.0)
                last.then_inc(s["col0"], 1)
                for c, tap in TAPS:
                    lag = DCONV - 1 - tap
                    if tap == DCONV - 2:
                        dve.wait_ge(s["ini"], b * EC + c + 1)
                    else:
                        dve.wait_ge(s["tap"], tap_at(b, c, tap + 1))
                    o = xc[:, c * T + lag:(c + 1) * T]
                    v.scalar_tensor_tensor(o, bank(c)[:, 0:T - lag], c_convw[:, c * DCONV + tap:c * DCONV + tap + 1],
                                           o, ALU.mult, ALU.add).then_inc(s["tap"], 1)

                def softplus(c):
                    dve.wait_ge(s["abs"], b * EC + SOFTPLUS_RANK[c] + 1)
                    v.tensor_scalar(sp_pos[c], bank(2 + c), c_bdt[:, c:c + 1], 0.0,
                                    ALU.add, ALU.max)
                    dve.wait_ge(s["e"], b * EC + SOFTPLUS_RANK[c] + 1)
                    low, e = sp_low[c], delta[:, c * T:(c + 1) * T]
                    self.link(v.tensor_scalar(low, e, 1.0, 1.0, ALU.add, ALU.subtract))
                    add_softplus(v, c, self.link, lambda: dve.wait_ge(s["ln"], b * EC + SOFTPLUS_RANK[c] + 1))\
                        .then_inc(s["dx"], 1)

                softplus(0)
                dve.wait_ge(s["bc"], b + 1)
                ps = bank(1)[0:96, :]
                self.link(v.tensor_copy(bc_hi[0:96, :], ps))
                v.tensor_copy(bc_stack[0:32, :], bc_hi[0:32, :])
                self.link(v.tensor_tensor(bc_rest[0:96, :], ps, bc_hi[0:96, :], ALU.subtract))
                self.link(v.tensor_copy(bc_mid[0:96, :], bc_rest[0:96, :]))
                v.tensor_copy(bc_stack[32:64, :], bc_mid[32:64, :])
                self.link(v.tensor_tensor(bc_rest[0:96, :], bc_rest[0:96, :], bc_mid[0:96, :], ALU.subtract))
                v.tensor_copy(bc_stack[64:96, :], bc_rest[64:96, :]).then_inc(s["stack"], 1)
                softplus(1)
                dve.wait_ge(s["dx"], (b + 1) * 2)

                def times_b(half, n, u):
                    at = (b * 2 + half) * DS + n
                    dve.wait_ge(s["B"], at + 1)
                    dve.wait_ge(s["scan"], HEAD + at - 3)
                    v.tensor_tensor(dbx[:, u * 2 * T:(u + 1) * 2 * T].rearrange("p (c t) -> p c t", c=2),
                                    dx[:, 2 * half * T:2 * (half + 1) * T].rearrange("p (c t) -> p c t", c=2),
                                    bank(u % 2).unsqueeze(1).broadcast_to([P, 2, T]), ALU.mult)\
                        .then_inc(s["mul"], 1)

                def scan(half, n, u):
                    at = (b * 2 + half) * DS + n
                    dve.wait_ge(s["dA"], at + 1)
                    dve.wait_ge(s["mul"], HEAD + at + 1)
                    dve.wait_ge(s["hc"], HEAD + at - 1)
                    v.tensor_tensor_scan(hst[:, (u % 2) * 2 * T:(u % 2 + 1) * 2 * T], decay[u % 2],
                                         dbx[:, u * 2 * T:(u + 1) * 2 * T], 0.0, ALU.mult, ALU.add)\
                        .then_inc(s["scan"], 1)

                def states(half, q, final=False):
                    for u in range(4):
                        if u < 3 or not final:
                            times_b(half, q * 4 + u + 1, (u + 1) % 4)
                        elif half == 0:
                            dve.wait_ge(s["dx_p"], (b + 1) * 2)
                            times_b(1, 0, 0)
                        scan(half, q * 4 + u, u)

                def finish(half):
                    dve.wait_ge(s["ys"], HEAD + (b * 2 + half + 1) * DS)
                    for j in range(2):
                        c = slice((2 * half + j) * T, (2 * half + j + 1) * T)
                        self.link(v.scalar_tensor_tensor(xc[:, c], xc[:, c], c_D[:, 2 * half + j:2 * half + j + 1],
                                                         bank(SUM_BANKS[half][j]), ALU.mult, ALU.add))
                        ins = v.tensor_tensor(zs[:, c], xc[:, c], zs[:, c], ALU.mult)
                        if half or j:
                            ins.then_inc(s["yf"], 1)

                quads = DS // 4
                times_b(0, 0, 0)
                with dve.Fori(0, quads - 1) as q:
                    states(0, q)
                states(0, quads - 1, final=True)
                states(1, 0)
                finish(0)
                with dve.Fori(1, quads - 1) as q:
                    states(1, q)
                states(1, quads - 1, final=True)
                self.norm(1 - b, it + 2, (s["hc"], HEAD + (b + 1) * 2 * DS))
                finish(1)
                self.norm_low(it + 2, 1 - b, banks=(0, 1))
                self.residual(it, b, 1.0)

            def attention(self, b):
                dve, v, s, it = self.dve, nc.vector, S[ATTN], 2 * ATTN + b
                v4 = v_four.rearrange("p (k j e) -> p k j e", k=TC, j=4)

                def rest(c, x, parts, part, needs):
                    dve.wait_ge(s["cast"], cast_at(b, c, needs))
                    x = x[:, c * T:(c + 1) * T]
                    v.tensor_tensor(x, x, part_of(parts, c, part), ALU.subtract).then_inc(s["rest"], 1)

                def queries(c):
                    dve.wait_ge(s["qkv"], b * 6 + 2 * c + 1)
                    v.tensor_scalar(q32[:, c * T:(c + 1) * T], bank(2 * c), c_bq[:, c:c + 1], HD ** -0.5,
                                    ALU.add, ALU.mult).then_inc(s["rest"], 1)

                queries(0)
                for c in range(DC):
                    rest(c, k32, k_parts, 0, "k_hi")
                    rest(c, q32, q_parts, 0, "q_hi")
                    rest(c, k32, k_parts, 1, "k_mid")
                    rest(c, q32, q_parts, 1, "q_mid")
                    if c == 0:
                        queries(1)
                        self.norm(1 - b, it + 2)
                self.link(v.memset(v_four, 0.0))
                v.memset(v4[:, :, :, HD:HD + 1], 1.0)

                def maxima(first, end):
                    with dve.Fori(first, end) as g:
                        for qc in range(TC):
                            n = (qc + 1) * P
                            dve.wait_ge(s["s1"], b * 32 + g * 4 + qc + 1)
                            v.reduce_max(m_all.rearrange("p (h c) -> p h c", c=TC)[:, bass.ds(g * 2, 2), qc],
                                         bank(2 * qc, 2).rearrange("p (j t) -> p j t", j=2)[:, :, 0:n], AX.X)\
                                .then_inc(s["max"], 1)

                for half in range(HALVES):
                    maxima(half * HH // 2, (half + 1) * HH // 2)
                    n = HH * TC
                    rest_of_m = m_rest[:, half * n:(half + 1) * n]
                    parts = [m_parts[:, (half * 3 + i) * n:(half * 3 + i + 1) * n] for i in range(3)]
                    dve.wait_ge(s["max"], HEAD + (b * 32 + (half + 1) * 16))
                    self.link(v.tensor_scalar(rest_of_m, m_all[:, half * n:(half + 1) * n], -1.0, None, ALU.mult))
                    for i in range(2):
                        self.link(v.tensor_copy(parts[i], rest_of_m))
                        self.link(v.tensor_tensor(rest_of_m, rest_of_m, parts[i], ALU.subtract))
                    v.tensor_copy(parts[2], rest_of_m).then_inc(s["mparts"], 1)

                def load_values(hq):
                    dve.wait_ge(s["vtok"], b * DC + DC)
                    dve.wait_ge(s["av"], HEAD + b * NH + hq * 4)
                    v.tensor_copy(v4[:, :, :, 0:HD],
                                  v_tok.rearrange("p (k f) -> p k f", k=TC)[:, :, bass.ds(hq * 4 * HD, 4 * HD)]
                                  .rearrange("p k (j e) -> p k j e", j=4)).then_inc(s["v4"], 1)

                def divide(hq):
                    dve.wait_ge(s["ot"], HEAD + b * 4 + hq + 1)
                    o = bank(7).rearrange("p (a e) -> p a e", e=32)
                    v.reciprocal(recip, o[:, :, HD]).then_inc(s["rc"], 1)
                    dve.wait_ge(s["rc"], b * 4 + hq + 1)
                    v.tensor_tensor(o_tok.rearrange("p (t f) -> p t f", t=TC)[:, :, bass.ds(hq * 4 * HD, 4 * HD)]
                                    .rearrange("p t (j e) -> p t j e", j=4),
                                    bank(7).rearrange("p (t j e) -> p t j e", t=TC, j=4)[:, :, :, 0:HD],
                                    recip.rearrange("p (t j) -> p t j", t=TC).unsqueeze(3)
                                    .broadcast_to([P, TC, 4, HD]), ALU.mult).then_inc(s["otok"], 1)

                load_values(0)
                with dve.Fori(0, NH // 4 - 1) as hq:
                    load_values(hq + 1)
                    divide(hq)
                divide(NH // 4 - 1)
                self.norm_low(it + 2, 1 - b, banks=(2, 3))
                self.residual(it, b, 1.0)

        def blocks(src, rows, width):
            out_, flat = [], []
            for k in range(width // P):
                for r in range(rows // P):
                    flat.append(src[:, r * width + k * P:r * width + (k + 1) * P])
            for g in range(0, len(flat), 4):
                out_.append([(i * P, P, f) for i, f in enumerate(flat[g:g + 4])])
            return out_

        PREP, PREP_DST = [], {}
        for name, rows, width, dst in (("W1", FH, D, W1T), ("W3", FH, D, W3T), ("Win", 2 * DI, D, WinT),
                                       ("Wx", DTR, DI, WxdT), ("Wdt", DI, DTR, WdtT), ("Wout", D, DI, WoutT),
                                       ("Wq", D, D, WqT), ("Wk", D, D, WkT), ("Wv", D, D, WvT), ("Wo", D, D, WoT)):
            groups = blocks(raw[name], rows, width)
            PREP.append((name, groups))
            split = isinstance(dst, tuple)
            PREP_DST[name] = [(P, (dst[0] if split else dst)[:, i * 512:(i + 1) * 512], None,
                               dst[1][:, i * 512:(i + 1) * 512] if split else None) for i in range(len(groups))]
        PREP.append(("Wxb", [[(k * 32, 32, raw["Wxb"][0:32, k * P:(k + 1) * P]) for k in range(EC)]]))
        PREP_DST["Wxb"] = [(P, WxbT.rearrange("p (k i c) -> p k i c", k=EC, i=3), "three", None)]
        PREP.append(("gate", [[(k * NE, NE, raw["gate"][0:NE, k * P:(k + 1) * P]) for k in range(DC)]]))
        PREP_DST["gate"] = [(P, gateT[:, 0:DC * NE], DC * NE, gateT[:, DC * NE:])]
        PREP.append(("vec", [[(0, VEC_ROWS, raw["vec"][0:VEC_ROWS, :])]]))
        PREP_DST["vec"] = [(P, cols[:, 16:16 + VEC_ROWS], VEC_ROWS, None)]
        PREP_LOAD = {n: n for n in ("W1", "W3", "Win", "Wdt", "Wout", "gate", "vec")}
        PREP_LOAD.update({"Wx": "Wx", "Wxb": "Wx", "Wq": "attn", "Wk": "attn", "Wv": "attn", "Wo": "attn"})
        PREP_COUNT = {n: 16 for n in PREP_LOAD}
        PREP_COUNT.update({"Wx": 32, "Wxb": 32, "Wq": 64, "Wk": 64, "Wv": 64, "Wo": 64, "vec": 16 * 6})

        def evacuation(src, dst):
            _, d, kind, _ = dst
            if kind == "three":
                src = src[:, 0:EC * 32].rearrange("p (k c) -> p k c", k=EC).unsqueeze(2).broadcast_to([P, EC, 3, 32])
            elif kind:
                src = src[:, 0:kind]
            return d, src

        flat = [(name, group, dst) for name, groups in PREP for group, dst in zip(groups, PREP_DST[name])]
        PREP_FIRST = [g for g in flat if g[0] in ("W1", "W3")]
        PREP_REST = [g for g in flat if g[0] not in ("W1", "W3")]
        REST_LOWS = [sum(g[2][3] is not None for g in PREP_REST[:n + 1]) for n in range(len(PREP_REST))]

        def side_bank(n):
            return bank((4, 7)[n % 2])

        def rest_groups(m, i):
            n = (m - 2) * 3 + i
            return (n,) if 2 <= m < FM and n < len(PREP_REST) else ()

        block = ctx.enter_context(nc.Block())

        @block.sync
        def _(sp):
            def rows_of(w, n=P):
                return w.rearrange("(r p) c -> p r c", p=n)

            def grid(t, r):
                return t.rearrange("p (r c) -> p r c", r=r)

            def load_x(b):
                sp.dma_start(x_tok[:, b * TC * D:(b + 1) * TC * D].rearrange("p (n d) -> p n d", d=D),
                             x[b].rearrange("(t p) d -> p t d", p=P)).then_inc(ld[f"x{b}"], 16)

            load_x(0)
            sp.dma_start(cf[:, :], const_f).then_inc(ld["const"], 16)
            sp.dma_start(grid(raw["W1"], FM), rows_of(W1)).then_inc(ld["W1"], 16)
            sp.dma_start(grid(raw["W3"], FM), rows_of(W3)).then_inc(ld["W3"], 16)
            sp.dma_start(grid(w2_raw, DC), rows_of(W2)).then_inc(ld["W2"], 16)
            load_x(1)
            sp.dma_start(grid(raw["Win"], FM), rows_of(W_in)).then_inc(ld["Win"], 16)
            sp.dma_start(raw["Wx"], W_x[0:DTR, :]).then_inc(ld["Wx"], 16)
            sp.dma_start(raw["Wxb"][0:32, :], W_x[DTR:DTR + 2 * DS, :]).then_inc(ld["Wx"], 16)
            sp.dma_start(grid(raw["Wdt"], EC), rows_of(W_dt)).then_inc(ld["Wdt"], 16)
            sp.dma_start(grid(raw["Wout"], DC), rows_of(W_out)).then_inc(ld["Wout"], 16)
            for name, w in (("Wq", Wq), ("Wk", Wk), ("Wv", Wv), ("Wo", Wo)):
                sp.dma_start(grid(raw[name], DC), rows_of(w)).then_inc(ld["attn"], 16)
            sp.wait_ge(down_done, 2 * MAMBA + 2)
            for dst, w, sw in ((w1s, w1, sw1), (w3s, w3, sw3)):
                for k in range(DC):
                    v = dst[:, k * MH:(k + 1) * MH]
                    sp.dma_start(v[:, 0:NE * EH].rearrange("p (e h) -> p e h", e=NE),
                                 w[:, k * P:(k + 1) * P, :].rearrange("e p h -> p e h")).then_inc(ld["moe"], 16)
                sp.dma_start(dst[:, :].rearrange("p (k h) -> p k h", k=DC)[:, :, NE * EH:MH],
                             sw.rearrange("(k p) h -> p k h", p=P)).then_inc(ld["moe"], 16)
            sp.dma_start(w2s[:, 0:RC * D].rearrange("p (m d) -> p m d", m=RC),
                         w2.rearrange("e h d -> (e h) d").rearrange("(m p) d -> p m d", p=P)).then_inc(ld["moe"], 16)
            sp.dma_start(w2s[:, RC * D:(RC + 1) * D], sw2[0:P, :]).then_inc(ld["moe"], 16)
            sp.dma_start(w2s[0:LAST_ROWS, (RC + 1) * D:MM * D], sw2[P:EH, :]).then_inc(ld["moe"], 16)
            sp.wait_ge(down_done, 2 * MOE0 + 2)
            sp.dma_start(k_stack[POS_ROW:STACK, :], aux_k).then_inc(ld["aux"], 16)
            sp.dma_start(q_stack[POS_ROW:MAX_ROW, :], aux_q).then_inc(ld["aux"], 16)

            def attention_moves(b):
                s = S[ATTN]
                sources = (("k", k_parts, scratch_k, k_stack), ("q", q_parts, scratch_q, q_stack))
                for c in range(DC):
                    for quad in (2 * c, 2 * c + 1):
                        sp.wait_ge(s[f"stacked{quad}"], b * 16 * 6)
                    for i, part in enumerate(("hi", "mid", "lo")):
                        for n, parts, scratch, _ in sources:
                            sp.wait_ge(s["cast"], cast_at(b, c, f"{n}_{part}"))
                            sp.dma_start(scratch[c, i].rearrange("d h t -> h d t"), part_of(parts, c, i))\
                                .then_inc(s[f"wrote{n}{c}"], 16)
                    for quad in range(2):
                        heads = slice((2 * c + quad) * 4 * T, (2 * c + quad + 1) * 4 * T)
                        own = slice(quad * 4, (quad + 1) * 4)
                        for n, _, scratch, stack in sources:
                            sp.wait_ge(s[f"wrote{n}{c}"], (b + 1) * 16 * 3)
                            sp.wait_ge(s["s2"], b * NH)
                            sp.wait_ge(down_done, 2 * ATTN + b)
                            row = 0
                            for part, slots in Q_RUNS:
                                if n == "k":
                                    src = scratch[c, 0:slots, :, own].rearrange("i d h t -> (i d) (h t)")
                                else:
                                    src = scratch[c, part:part + 1, :, own].rearrange("i d h t -> i d (h t)")\
                                        .broadcast_to([slots, HD, 4 * T])
                                sp.dma_start(stack[row:row + slots * HD, heads], src)\
                                    .then_inc(s[f"stacked{2 * c + quad}"], 16)
                                row += slots * HD
                for half in range(HALVES):
                    sp.wait_ge(s["mrows"], b * HALVES + half + 1)
                    sp.dma_start(scratch_m[half], m_rows[0:3 * HH * TC, half * P:(half + 1) * P])\
                        .then_inc(s[f"mwrote{half}"], 16)
                    sp.wait_ge(s[f"mwrote{half}"], (b + 1) * 16)
                    sp.dma_start(q_stack[MAX_ROW:STACK, half * HH * T:(half + 1) * HH * T],
                                 scratch_m[half].rearrange("(i a) q -> i (a q)", i=3))\
                        .then_inc(s[f"mstacked{half}"], 16)

            over_batches(sp, attention_moves, peeled=True)
            for b in range(NB):
                sp.wait_ge(resid_done, HEAD + 2 * MOE1 + b + 1)
                sp.dma_start(out[b].rearrange("(t p) d -> p t d", p=P),
                             x_tok[:, b * TC * D:(b + 1) * TC * D].rearrange("p (t d) -> p t d", d=D))\
                    .then_inc(stored, 16)
            sp.wait_ge(stored, 32)

        @block.gpsimd
        def _(pool):
            def mamba(b):
                s = S[MAMBA]
                for i, c in enumerate(SOFTPLUS_POOL):
                    links = [(b * 2 + i) * 3]

                    def link(ins):
                        links[0] += 1
                        ins.then_inc(s["sp"], 1)
                        pool.wait_ge(s["sp"], links[0])

                    pool.wait_ge(s["u"], b * 4 + (2 * i + 2))
                    add_softplus(nc.gpsimd, c, link, lambda: pool.wait_ge(s["ln"], b * EC + SOFTPLUS_RANK[c] + 1))\
                        .then_inc(s["dx_p"], 1)
                with pool.Fori(0, 2 * DS // 4) as q:
                    for u in range(4):
                        at = b * 2 * DS + q * 4 + u
                        pool.wait_ge(s["scan"], HEAD + at + 1)
                        pool.wait_ge(s["cev"], HEAD + at + 1)
                        pool.wait_ge(s["ys"], HEAD + at - 3)
                        nc.gpsimd.tensor_tensor(
                            hc[:, u * 2 * T:(u + 1) * 2 * T].rearrange("p (c t) -> p c t", c=2),
                            hst[:, (u % 2) * 2 * T:(u % 2 + 1) * 2 * T].rearrange("p (c t) -> p c t", c=2),
                            c_bc[:, (u % 2) * T:(u % 2 + 1) * T].unsqueeze(1).broadcast_to([P, 2, T]),
                            ALU.mult).then_inc(s["hc"], 1)

            zero = cols[:, 49:50]
            halved = [0]

            def halve(pieces):
                for src, hi, lo in pieces:
                    z = zero[0:src.shape[0]]
                    z = (z.unsqueeze(1) if len(src.shape) == 3 else z).broadcast_to(list(src.shape))
                    last = nc.gpsimd.tensor_tensor(hi, src, z, ALU.add)
                last.then_inc(moe_hi, 1)
                halved[0] += 1
                pool.wait_ge(moe_hi, halved[0])
                for src, hi, lo in pieces:
                    last = nc.gpsimd.tensor_tensor(lo, src, hi, ALU.subtract)
                return last

            def rows_of_chunk(m):
                return LAST_ROWS if m == MM - 1 else P

            def halve_up(p):
                m = MOE_ORDER[p]

                def part(t):
                    return t.rearrange("p (k h) -> p k h", k=DC)[:, :, m * P:m * P + rows_of_chunk(m)]

                halve([(part(w), part(h[0]), part(h[1])) for w, h in ((w1s, w1h), (w3s, w3h))]).then_inc(moe_split, 1)

            def halve_down(p):
                m = MOE_ORDER[p]
                return halve([tuple(t[0:rows_of_chunk(m), m * D:(m + 1) * D] for t in (w2s, w2_hi, w2_lo))])

            def halve_others():
                for p in range(MM):
                    last = halve_down(p)
                    if p + 2 < MM:
                        halve_up(p + 2)
                last.then_inc(moe_split, 1)

            start_heads(pool, "POOL")
            over_batches(pool, mamba)
            pool.wait_ge(col_ready, 1)
            pool.wait_ge(ld["moe"], 16 * MOE_LOADS)
            pool.wait_ge(S[FFN1]["up"], NB * FM)
            halve_up(0)
            halve_up(1)
            pool.wait_ge(down_done, 2 * FFN1 + 2)
            halve_others()
            s = S[ATTN]
            pool.wait_ge(s["s2"], NB * NH)
            pool.wait_ge(s["av"], HEAD + NB * NH)
            pool.wait_ge(s["v4"], NB * 4)
            halve_up(0)
            halve_up(1)
            halve_others()

        @block.scalar
        def _(act):
            act.dma_start(cb[:, :], const_b).then_inc(ld["const"], 16)
            act.dma_start(raw["gate"][0:NE, :], gate_w).then_inc(ld["gate"], 16)
            act.dma_start(bo_row[0:1, :], bo.rearrange("(a n) -> a n", a=1)).then_inc(ld["bo"], 16)
            at = 0
            for v in (conv_b, b_dt, Dp, bq, bk, bv):
                n = v.shape[0] // P
                act.dma_start(raw["vec"][at:at + n, :], v.rearrange("(c p) -> c p", p=P)).then_inc(ld["vec"], 16)
                at += n
            act.dma_start(c_convw.rearrange("p (c k) -> p c k", c=EC), conv_w.rearrange("(c p) k -> p c k", p=P))\
                .then_inc(ld["cols"], 16)
            act.dma_start(c_A.rearrange("p (c s) -> p c s", c=EC), A_log.rearrange("(c p) s -> p c s", p=P))\
                .then_inc(ld["cols"], 16)
            start_heads(act, "ACT")
            prog = ScalarProgram(act)
            prog.prepare()
            over_batches(act, lambda b: prog.ffn(FFN0, b), peeled=True)
            over_batches(act, prog.mamba)
            over_batches(act, lambda b: prog.ffn(FFN1, b))
            over_batches(act, lambda b: prog.moe(MOE0, b))
            over_batches(act, prog.attention)
            over_batches(act, lambda b: prog.moe(MOE1, b), peeled=True)

        @block.vector
        def _(dve):
            start_heads(dve, "DVE")
            prog = VectorProgram(dve)
            prog.prepare()
            prog.base = prog.n
            prog.stage(lambda b: prog.ffn(FFN0, b), 3, peeled=True)
            prog.stage(prog.mamba, 19)
            prog.stage(lambda b: prog.ffn(FFN1, b), 3)
            prog.stage(lambda b: prog.moe(MOE0, b), 20)
            prog.stage(prog.attention, 14)
            prog.stage(lambda b: prog.moe(MOE1, b), 20, peeled=True)

        @block.tensor
        def _(pe):
            start_heads(pe, "PE")
            prog = TensorProgram(pe)
            prog.prepare()
            over_batches(pe, lambda b: prog.ffn(FFN0, b), peeled=True)
            over_batches(pe, prog.mamba)
            over_batches(pe, lambda b: prog.ffn(FFN1, b))
            over_batches(pe, lambda b: prog.moe(MOE0, b))
            pe.wait_ge(ld["bo"], 16)
            pe.wait_ge(col_ready, 1)
            over_batches(pe, prog.attention)
            over_batches(pe, lambda b: prog.moe(MOE1, b), peeled=True)


_INS = ['L0_attn_x', 'L0_attn_W_in', 'L0_attn_conv_w', 'L0_attn_conv_b', 'L0_attn_W_x', 'L0_attn_W_dt',
        'L0_attn_b_dt', 'L0_attn_A_log', 'L0_attn_Dp', 'L0_attn_W_out', 'L0_ffn_W1', 'L0_ffn_W2', 'L0_ffn_W3',
        'L1_attn_Wq', 'L1_attn_bq', 'L1_attn_Wk', 'L1_attn_bk', 'L1_attn_Wv', 'L1_attn_bv', 'L1_attn_Wo',
        'L1_attn_bo', 'L1_ffn_gate_w', 'L1_ffn_w1', 'L1_ffn_w2', 'L1_ffn_w3', 'L1_ffn_sw1', 'L1_ffn_sw2',
        'L1_ffn_sw3']


def _constants():
    def bf16(v):
        return (np.ascontiguousarray(v, dtype=np.float32).view(np.uint32) >> 16).astype(np.uint16)

    def parts(v):
        res, rest = [], np.asarray(v, np.float32)
        for _ in range(3):
            hi = (rest.view(np.uint32) & 0xFFFF0000).view(np.float32)
            res.append(hi)
            rest = (rest - hi).astype(np.float32)
        return res

    f = np.zeros((P, CF_COLS), np.float32)
    i = np.arange(P)
    f[:, 0:128] = np.eye(P)
    bits = i[:, None] & i[None, :]
    parity = sum((bits >> s) & 1 for s in range(7)) % 2
    f[:, 128:256] = (1 - 2 * parity) / 32.0
    e = np.arange(NE)
    f[:, 256:320] = (e[None, :] < e[:, None]).reshape(1, -1)

    c = np.zeros((P, CB_COLS), np.float32)
    c[:, 0:128] = np.eye(P)
    c[:, 128:256] = np.where(i[None, :] > i[:, None], -2.0 ** 100, 0)
    c[:, 256:384] = np.where(i[:, None] > i[None, :], -2.0 ** 100, 0)
    for r in range(96):
        c[r, 384 + r % 32] = 1
    for r in range(RC * P):
        for part in range(3):
            c[part * NE + r // EH, CB["expert"][0] + r] = 1

    start = 2.0 ** (-2.0 ** (-(np.log2(NH) - 3)))
    slope = parts(np.array([start * start ** h for h in range(NH)], np.float32))
    pos = np.arange(T)
    halves = [(pos // P * P).astype(np.float32), (pos % P).astype(np.float32)]
    aux_q, aux_k = np.zeros((12, NH, T), np.float32), np.zeros((15, NH, T), np.float32)
    r = 0
    for sp in slope:
        for hv in halves:
            aux_q[r], aux_k[r] = sp[:, None], hv[None, :]
            aux_q[r + 6], aux_k[r + 6] = -hv[None, :], sp[:, None]
            r += 1
    aux_k[12:15] = 1
    return {"const_f": f, "const_b": bf16(c), "aux_q": bf16(aux_q.reshape(12, -1)),
            "aux_k": bf16(aux_k.reshape(15, -1))}


def kernel(**inputs):
    import concourse.bacc as _bacc
    from concourse.bass_utils import run_bass_kernel_spmd as _run

    nc = _bacc.Bacc("TRN2", target_bir_lowering=False, num_devices=1)
    arrays, args = {}, []
    for name in _INS:
        a = np.ascontiguousarray(inputs[name])
        arrays[f"in_{name}_dram"] = a
        args.append(nc.dram_tensor(f"in_{name}_dram", a.shape, mybir.dt.from_np(a.dtype), kind="ExternalInput").ap())
    for name, a in _constants().items():
        arrays[name] = a
        ap = nc.dram_tensor(name, a.shape, mybir.dt.from_np(a.dtype), kind="ExternalInput").ap()
        args.append(ap if a.dtype == np.float32 else ap.bitcast(BF16))
    out = nc.dram_tensor("out_dram", (NB, T, D), F32, kind="ExternalOutput").ap()
    build(nc, *args, out)
    r = _run(nc, [arrays], core_ids=[0])
    return r.results[0]["out_dram"]
```
